# Optimizing a Trainium2 kernel written in Bass

```python
import numpy as np
import jax
import jax.numpy as jnp

def _softmax(x, axis=-1):
    return jax.nn.softmax(x, axis=axis)

def _gelu(x):
    return jax.nn.gelu(x, approximate=True)

def _silu(x):
    return jax.nn.silu(x)

def _sigmoid(x):
    return jax.nn.sigmoid(x)

def _layernorm(x, axis=-1, eps=1e-05):
    m = jnp.mean(x, axis=axis, keepdims=True)
    v = jnp.var(x, axis=axis, keepdims=True)
    return (x - m) / jnp.sqrt(v + eps)

def _scatter_add(tgt, idx, src, axis=0):
    return tgt.at[idx].add(src)

def _segment_sum(src, seg, n):
    return jax.ops.segment_sum(src, seg, n)
kernel_name = 'mk_macaron_d1_jaxref_r4_4d6a34'

def setup_inputs(seed: int=0):
    np.random.seed(seed)
    _w = jnp.asarray

    def _L0_attn_setup():
        import jax, jax.numpy as jnp
        import numpy as np
        B, T, D = (8, 1024, 256)
        key = jax.random.key(seed)
        ks = jax.random.split(key, 7)
        s1 = 1.0 / np.sqrt(D)
        return {'x': jax.random.normal(ks[0], (B, T, D), dtype=jnp.float32), 'W1': jax.random.normal(ks[1], (D, D), dtype=jnp.float32) * s1, 'b1': jnp.zeros((D,), dtype=jnp.float32), 'w2': jax.random.normal(ks[2], (1, D), dtype=jnp.float32) * s1, 'b2': jnp.zeros((1,), dtype=jnp.float32), 'Wc': jax.random.normal(ks[3], (D, 2 * D), dtype=jnp.float32) * (1.0 / np.sqrt(2 * D)), 'bc': jnp.zeros((D,), dtype=jnp.float32)}
    _L0_attn_in = _L0_attn_setup()

    def _L0_ffn_setup():
        import jax, jax.numpy as jnp
        import numpy as np

        def _bitlinear(x, w_latent):
            scale = jax.lax.stop_gradient(jnp.clip(jnp.mean(jnp.abs(w_latent), axis=1, keepdims=True), 1e-05, None))
            tern = jnp.clip(jnp.round(w_latent / scale), -1.0, 1.0)
            w = w_latent + jax.lax.stop_gradient(tern - w_latent)
            return x @ (w * scale).T
        key = jax.random.key(seed)
        ks = jax.random.split(key, 6)
        dim, hidden, rank = (256, 1024, 16)
        B, S = (4, 1024)
        x = jax.random.normal(ks[0], (B, S, dim), dtype=jnp.float32)
        w_fc = 0.02 * jax.random.normal(ks[1], (hidden, dim), dtype=jnp.float32)
        w_proj = 0.02 * jax.random.normal(ks[2], (dim, hidden), dtype=jnp.float32)
        u = 0.02 * jax.random.normal(ks[3], (hidden, rank), dtype=jnp.float32)
        v = 0.02 * jax.random.normal(ks[4], (rank, dim), dtype=jnp.float32)
        fast_b = jax.random.normal(ks[5], (rank, rank), dtype=jnp.float32)
        gate = jnp.float32(0.05)
        return {'x': x, 'fast_b': fast_b, 'w_fc': w_fc, 'w_proj': w_proj, 'u': u, 'v': v, 'gate': gate}
    _L0_ffn_in = _L0_ffn_setup()
    _d = {'L0_attn_x': _L0_attn_in['x'], 'L0_attn_W1': _L0_attn_in['W1'], 'L0_attn_b1': _L0_attn_in['b1'], 'L0_attn_w2': _L0_attn_in['w2'], 'L0_attn_b2': _L0_attn_in['b2'], 'L0_attn_Wc': _L0_attn_in['Wc'], 'L0_attn_bc': _L0_attn_in['bc'], 'L0_ffn_fast_b': _L0_ffn_in['fast_b'], 'L0_ffn_w_fc': _L0_ffn_in['w_fc'], 'L0_ffn_w_proj': _L0_ffn_in['w_proj'], 'L0_ffn_u': _L0_ffn_in['u'], 'L0_ffn_v': _L0_ffn_in['v'], 'L0_ffn_gate': _L0_ffn_in['gate']}
    _x0 = _d['L0_attn_x']
    _d['L0_attn_x'] = jax.random.normal(jax.random.fold_in(jax.random.key(seed), 1), (8, 1024, 256), dtype=_x0.dtype)
    del _x0
    return _d

def reference(L0_attn_x, L0_attn_W1, L0_attn_b1, L0_attn_w2, L0_attn_b2, L0_attn_Wc, L0_attn_bc, L0_ffn_fast_b, L0_ffn_w_fc, L0_ffn_w_proj, L0_ffn_u, L0_ffn_v, L0_ffn_gate):

    def _L0_attn_ref(x, W1, b1, w2, b2, Wc, bc):
        import jax, jax.numpy as jnp
        import numpy as np
        B, T, D = (8, 1024, 256)
        h = jnp.tanh(jnp.einsum('btd,ed->bte', x, W1) + b1)
        s = (jnp.einsum('btd,od->bto', h, w2) + b2)[..., 0]
        m = jnp.max(s, axis=1, keepdims=True)
        e = jnp.exp(s - m)
        num = jnp.cumsum(e[..., None] * x, axis=1)
        den = jnp.cumsum(e, axis=1)[..., None]
        ctx = num / den
        combined = jnp.concatenate((ctx, x), axis=2)
        out = jnp.tanh(jnp.einsum('btk,dk->btd', combined, Wc) + bc)
        return out

    def _L0_ffn_ref(x, fast_b, w_fc, w_proj, u, v, gate):
        import jax, jax.numpy as jnp
        import numpy as np

        def _bitlinear(x, w_latent):
            scale = jax.lax.stop_gradient(jnp.clip(jnp.mean(jnp.abs(w_latent), axis=1, keepdims=True), 1e-05, None))
            tern = jnp.clip(jnp.round(w_latent / scale), -1.0, 1.0)
            w = w_latent + jax.lax.stop_gradient(tern - w_latent)
            return x @ (w * scale).T
        h = _bitlinear(x, w_fc) + gate * (x @ v.T @ fast_b.T @ u.T)
        r = jnp.maximum(h, 0.0)
        return _bitlinear(r * r, w_proj)
    x = L0_attn_x
    x = x + 0.5 * _L0_ffn_ref(_layernorm(x, axis=-1), L0_ffn_fast_b, L0_ffn_w_fc, L0_ffn_w_proj, L0_ffn_u, L0_ffn_v, L0_ffn_gate)
    x = x + _L0_attn_ref(_layernorm(x, axis=-1), L0_attn_W1, L0_attn_b1, L0_attn_w2, L0_attn_b2, L0_attn_Wc, L0_attn_bc)
    x = x + 0.5 * _L0_ffn_ref(_layernorm(x, axis=-1), L0_ffn_fast_b, L0_ffn_w_fc, L0_ffn_w_proj, L0_ffn_u, L0_ffn_v, L0_ffn_gate)
    return x

_drawn_inputs = setup_inputs


def setup_inputs(seed=0):
    import zlib

    import numpy as np

    out = dict(_drawn_inputs(seed))
    spreads = {'L0_attn_b1': (0.0, 2.0), 'L0_attn_bc': (0.0, 0.279)}
    factors = {'L0_ffn_fast_b': 8.0, 'L0_ffn_u': 8.0, 'L0_ffn_v': 8.0, 'L0_attn_W1': 13.175}
    for name, (base, spread) in spreads.items():
        noise = np.random.default_rng([zlib.crc32(name.encode()), seed]).standard_normal(out[name].shape)
        drawn = base * np.exp(spread * noise) if base else spread * noise
        out[name] = jnp.asarray(drawn.astype(out[name].dtype))
    for name, factor in factors.items():
        out[name] = (out[name] * factor).astype(out[name].dtype)
    return out
```

```python
from contextlib import ExitStack

import concourse.bass as bass
from concourse import mybir

F32 = mybir.dt.float32
F32R = mybir.dt.float32r
ALU = mybir.AluOpType
ACT = mybir.ActivationFunctionType
AX_X = mybir.AxisListType.X
RMAX = bass.bass_isa.ReduceOp.max

P = 128
B, T, D = 8, 1024, 256
PRIMED = 1
H, R = 1024, 16
KT = D // P
HT = H // P
G = 512
GC = G // P
CH = T // P
EPS = 1e-5
NY = D + 2

LAG = 2
LAST_SLOT = 4 * HT + LAG
GROUP_AT = {0: ("A", 0), HT: ("A", 1), 2 * HT: ("D", 0), 3 * HT: ("D", 1)}
SLOTS = {s: [] for s in range(LAST_SLOT)}
SLOTS[0] += [("stats", "A", 1)]
SLOTS[1] += [("exp", "C", 0)]
SLOTS[2] += [("norm", "A", 1)]
SLOTS[3] += [("turn", "A", 1)]
SLOTS[5] += [("z", "A", 1)]
for _c in range(CH):
    SLOTS[2 * _c + 1] += [("mix", "C", _c)]
    SLOTS[2 * _c + 2] += [("sum", "C", _c)]
    if _c < CH - 1:
        SLOTS[2 * _c + 3] += [("carry", "C", _c)]
SLOTS[10] += [("stats", "D", 0)]
SLOTS[11] += [("load", "A", 0), ("norm", "D", 0), ("stats", "B", 0)]
SLOTS[12] += [("turn", "D", 0)]
SLOTS[13] += [("norm", "B", 0)]
SLOTS[14] += [("turn", "B", 0), ("z", "D", 0)]
SLOTS[16] += [("hidden", "B", 0, 0)]
SLOTS[18] += [("hidden", "B", 0, 1), ("stats", "D", 1)]
SLOTS[19] += [("load", "A", 1), ("score", "B", 0), ("norm", "D", 1), ("stats", "B", 1)]
SLOTS[20] += [("turn", "D", 1)]
SLOTS[21] += [("norm", "B", 1)]
SLOTS[22] += [("z", "D", 1)]
SLOTS[23] += [("turn", "B", 1)]
SLOTS[26] += [("stats", "N", 0)]
SLOTS[27] += [("norm", "N", 0)]
SLOTS[28] += [("hidden", "B", 1, 0)]
SLOTS[29] += [("turn", "N", 0)]
SLOTS[32] += [("hidden", "B", 1, 1)]
SLOTS[33] += [("z", "N", 0), ("score", "B", 1), ("peak", "B", 0)]


class Num:

    def __init__(self, first, each=0, i=None):
        self.first, self.each, self.i = first, each, i

    def __add__(self, n):
        if isinstance(n, Num):
            return Num(self.first + n.first, self.each + n.each, self.i or n.i)
        return Num(self.first + n, self.each, self.i)

    def __sub__(self, n):
        return self + (-n)

    def __rmul__(self, n):
        return Num(n * self.first, n * self.each, self.i)

    def ring(self, m):
        assert self.each % m == 0
        return self.first % m

    @property
    def value(self):
        return self.first if self.each == 0 else self.first + self.each * self.i


def wait(eng, sem, n):
    if n.each == 0 and n.first <= 0:
        return
    assert n.first >= 0, (sem, n.first)
    eng.wait_ge(sem, (n + PRIMED).value)


def wait_apart(eng, passed, *waits):
    if all(n.each == 0 for _, n in waits):
        for sem, n in waits:
            wait(eng, sem, n)
        return
    values = [eng.to_reg((n + PRIMED).value) for _, n in waits]
    eng.wait_ge(*passed)
    for (sem, _), value in zip(waits, values):
        eng.wait_ge(sem, value)


class Step:

    def __init__(self, name, kind=None, half=None, c=None, j=None, e=None, group=None, tile=None,
                 chunk=None, chunks=None, number=None, batch=None, prep=None, base=None, mixed=None,
                 bank=None, before=None):
        self.name, self.kind, self.half = name, kind, half
        self.c, self.j, self.e = c, j, e
        self.group, self.tile = group, tile
        self.chunk, self.chunks = chunk, chunks
        self.number = number
        self.batch, self.prep = batch, prep
        self.base, self.mixed = base, mixed
        self.bank, self.before = bank, before


def keeps(part, phase):
    return {"first": phase in "ABN", "full": True, "last full": phase != "N", "end": phase in "CD"}[part]


def steps_of(part, before, i=None, each=None):
    at = {k: Num(v, (each or {}).get(k, 0), i) for k, v in before.items()}
    out = []
    turn_of = {}

    def take(kind, n=1):
        now = at[kind]
        at[kind] = now + n
        return now

    def group_of(phase, half):
        if phase == "N":
            return at["batch group"] + per_batch
        return at["batch group"] + (half if phase == "A" or part == "end" else 2 + half)

    per_batch = {"first": 2, "full": 4, "last full": 4, "end": 2}[part]

    uses = [None, None] if part == "first" else [
        Step("hidden", number=4 * at["a batch"] - 1) if part == "end" else Step("z", group=at["batch group"]),
        Step("score", number=2 * at["a batch"] - 1)]

    def on_bank(step):
        step.bank, step.before = take("item").ring(2), uses[-2]
        uses.append(step)
        return step

    slots = range(-1, LAST_SLOT) if part == "first" else range(LAST_SLOT)
    tiles = {}
    for s0, (phase, half) in GROUP_AT.items():
        if keeps(part, phase):
            for j in range(HT):
                tiles[s0 + j] = (phase, half, j)
    for s in slots:
        todo = SLOTS[s] if s >= 0 else [("load", "F", 0), ("load", "F", 1), ("stats", "F", 0), ("norm", "F", 0), ("turn", "F", 0), ("z", "F", 0)]
        if s in tiles:
            phase, half, j = tiles[s]
            g = group_of(phase, half)
            out.append(on_bank(Step("up", group=g, tile=HT * g + j, j=j)))
        for name, phase, *rest in todo:
            if phase != "F" and not keeps(part, phase):
                continue
            half = rest[0]
            kind = "A" if phase in "NF" else phase
            if name == "load":
                if phase == "F" or keeps(part, "N"):
                    batch = at["a batch"] if phase == "F" else at["a batch"] + 1
                    g = None if phase == "F" else group_of("A", half)
                    out.append(Step("load", half=half, batch=batch, group=g))
            elif name == "norm":
                out.append(Step("norm", kind=kind, half=half, prep=take("norm")))
            elif name == "stats":
                src = {"A": at["a batch"] + (1 if phase == "N" else 0), "B": None, "D": None}[kind]
                out.append(Step("stats", kind=kind, half=half, prep=take("prep"), batch=src,
                                group=group_of("A", half) if kind == "B" else None,
                                chunks=CH * at["c batch"] + GC * (half + 1)))
            elif name == "turn":
                q = take("turn")
                turn_of[phase, half] = q
                g = None if kind == "B" else (Num(0) if phase == "F" else group_of(phase, half))
                out.append(Step("turn", kind=kind, half=half, prep=q, group=g))
            elif name == "z":
                g = Num(0) if phase == "F" else group_of(phase, half)
                out.append(on_bank(Step("z", group=g, prep=turn_of[phase, half])))
            elif name == "hidden":
                e = rest[1]
                out.append(on_bank(Step("hidden", half=half, e=e, number=2 * (2 * at["a batch"] + half) + e,
                                        prep=turn_of["B", half])))
            elif name == "score":
                out.append(on_bank(Step("score", half=half, number=2 * at["a batch"] + half,
                                        batch=at["a batch"])))
            elif name == "peak":
                out.append(Step("peak", batch=at["a batch"]))
            elif name == "exp":
                out.append(Step("exp", batch=at["c batch"]))
            else:
                c = rest[0]
                out.append(Step(name, c=c, chunk=CH * at["c batch"] + c, batch=at["c batch"],
                                base=at["batch group"]))
        if s - LAG in tiles:
            phase, half, j = tiles[s - LAG]
            g = group_of(phase, half)
            out.append(Step("down", group=g, tile=HT * g + j, j=j))
            if j == HT - 1:
                out.append(Step("land", kind=phase, half=half, group=g, batch=at["c batch"],
                                mixed=Num(0) if part == "first" else CH * at["c batch"] + GC * (half + 1)))
    at["batch group"] += per_batch
    at["a batch"] += 1
    if part != "first":
        at["c batch"] += 1
    return out, {k: v.first for k, v in at.items()}


ZERO = {"item": 0, "prep": 0, "norm": 0, "turn": 0, "batch group": 0, "a batch": 0, "c batch": 0}
FULL_TURNS = B - 2


def program_parts():
    _, after_first = steps_of("first", ZERO)
    _, after_one = steps_of("full", after_first)
    each = {k: after_one[k] - after_first[k] for k in after_one}
    after_loop = {k: after_first[k] + FULL_TURNS * each[k] for k in each}
    _, after_last = steps_of("last full", after_loop)
    return [("first", ZERO), ("full", after_first), ("last full", after_loop), ("end", after_last)], each


def run_parts(eng, do):
    parts, each = program_parts()
    for part, before in parts:
        if part == "full":
            with eng.Fori(0, FULL_TURNS) as i:
                do(steps_of(part, before, i, each)[0], part)
        else:
            do(steps_of(part, before)[0], part)


def macaron(nc, x, W1, b1, w2, b2, Wc, bc, fast_b, w_fc, w_proj, u, v, gate, out):
    ctx = ExitStack()
    with ctx:
        def sb(name, shape, dt=F32):
            return ctx.enter_context(nc.sbuf_tensor(name, shape, dt))

        def sem(name):
            return ctx.enter_context(nc.semaphore(name))

        counting = []

        def count(name):
            counting.append(sem(name))
            return counting[-1]

        fcT = sb("fcT", [P, KT, H], F32R)
        projT = sb("projT", [P, HT, D], F32R)
        U = sb("U", [P, H], F32R)
        V = sb("V", [P, KT, P], F32R)
        W1T = sb("W1T", [P, KT, D])
        WcT = sb("WcT", [P, KT, 2 * D])
        fc_scale = sb("fc_scale", [P, HT])
        proj_row = sb("proj_row", [P, 2, D])
        b1c = sb("b1c", [P, KT])
        w2c = sb("w2c", [P, KT])
        bcb = sb("bcb", [P, D])
        b2b = sb("b2b", [P, 1])
        gateb = sb("gateb", [P, 1])
        ident = sb("ident", [P, P])
        ones = sb("ones", [P, P])
        tri_f = sb("tri_f", [P, P])
        tri = sb("tri", [P, P], F32R)
        rest = sb("rest", [P, P], F32R)
        exponent = sb("exponent", [P, GC])

        fc_in = sb("fc_in", [P, HT, D])
        proj_in = sb("proj_in", [P, KT, H])
        W1_in = sb("W1_in", [P, KT, D])
        Wc_in = sb("Wc_in", [P, KT, 2 * D])
        u_in = sb("u_in", [P, HT, R])
        v_in = sb("v_in", [R, D])
        fbT_in = sb("fbT_in", [R, R])
        fc_sum = sb("fc_sum", [P, HT])
        fc_half = sb("fc_half", [P, HT])
        fc_nhalf = sb("fc_nhalf", [P, HT])
        fc_inv = sb("fc_inv", [P, HT])
        proj_sum = sb("proj_sum", [P, KT])
        proj_half = sb("proj_half", [P, KT])
        proj_nhalf = sb("proj_nhalf", [P, KT])
        proj_wide = sb("proj_wide", [P, KT, P])
        below = sb("below", [P, H])
        us = sb("us", [P, HT, R])
        uh = sb("uh", [P, HT, R], F32R)
        ul = sb("ul", [P, HT, R], F32R)
        u_nat = sb("u_nat", [P, HT, P])
        vf = sb("vf", [P, KT, R])
        vh = sb("vh", [P, KT, R], F32R)

        X0 = [sb(f"X0_{h}", [P, GC, D]) for h in range(2)]
        XA = [sb(f"XA_{h}", [P, GC, D]) for h in range(2)]
        XB = [sb(f"XB_{h}", [P, GC, D]) for h in range(2)]
        XO = [sb(f"XO_{h}", [P, GC, D]) for h in range(2)]
        bn = sb("bn", [P, GC, 6])
        moments = sb("moments", [P, GC, 2])
        var_eps = sb("var_eps", [P, GC])
        rstd = sb("rstd", [P, GC])
        xn = [sb(f"xn{n}", [P, GC, D]) for n in range(2)]
        xh = [sb(f"xh{n}", [P, KT, G], F32R) for n in range(2)]
        xl = [sb(f"xl{n}", [P, KT, G], F32R) for n in range(2)]
        zt = [sb(f"zt{n}", [P, G], F32R) for n in range(2)]
        r = [sb(f"r{n}", [P, G]) for n in range(2)]
        sq = [sb(f"sq{n}", [P, G]) for n in range(2)]
        r2h = [sb(f"r2h{n}", [P, G], F32R) for n in range(4)]
        r2l = [sb(f"r2l{n}", [P, G], F32R) for n in range(4)]
        ffn = [sb(f"ffn{n}", [P, 2, D]) for n in range(2)]
        xnT = sb("xnT", [P, KT, T])
        hT = sb("hT", [P, KT, G])
        s_all = sb("s_all", [P, CH])
        row_max = sb("row_max", [P, 1])
        peak = sb("peak", [P, 1])
        minus_peak = sb("minus_peak", [P, 1])
        e = sb("e", [P, CH])
        yh = sb("yh", [P, CH, NY], F32R)
        yl = sb("yl", [P, CH, NY], F32R)
        own = [sb(f"own{n}", [P, D]) for n in range(2)]
        rden = sb("rden", [P, 1])
        pre = [sb(f"pre{n}", [P, D]) for n in range(2)]
        th = [sb(f"th{n}", [P, D]) for n in range(2)]

        bank = [ctx.enter_context(nc.psum_tensor(f"bank{n}", [P, 512], F32)) for n in range(8)]
        work, acc, turned_bank, mix_bank, sum_bank = bank[0:2], bank[2:4], bank[4:6], bank[6], bank[7]

        w_loaded, x_loaded = sem("w_loaded"), [count(f"x_loaded{h}") for h in range(2)]
        stored = [count(f"stored{h}") for h in range(2)]
        const_done, dve_prep, act_prep, pe_prep, pool_prep, copy_prep, vector_chain = (
            sem("const_done"), sem("dve_prep"), sem("act_prep"), sem("pe_prep"), sem("pool_prep"),
            sem("copy_prep"), sem("vector_chain"))
        stats_done, moments_done, var_done, rstd_done, xn_ready = (
            count("stats_done"), count("moments_done"), count("var_done"), count("rstd_done"), count("xn_ready"))
        turned, hi_done, turn_taken = count("turned"), count("hi_done"), count("turn_taken")
        z_done, zh_done, zl_done = count("z_done"), count("zh_done"), count("zl_done")
        up_done, relu_done, r2h_done, sq_done, r2l_done = (
            count("up_done"), count("relu_done"), count("r2h_done"), count("sq_done"), count("r2l_done"))
        down_done, landed, added = count("down_done"), count("landed"), count("added")
        hid_done, tanh_done, score_done, scored = (
            count("hid_done"), count("tanh_done"), count("score_done"), count("scored"))
        rowmax_done, peak_done, minus_peak_done = count("rowmax_done"), count("peak_done"), count("minus_peak_done")
        exp_done, eh_done, el_done = count("exp_done"), count("eh_done"), count("el_done")
        mix_done, yh_done, yl_done, own_done = count("mix_done"), count("yh_done"), count("yl_done"), count("own_done")
        sum_done, rden_done, pre_done, gate_done, x2_ready = (
            count("sum_done"), count("rden_done"), count("pre_done"), count("gate_done"), count("x2_ready"))

        block = ctx.enter_context(nc.Block())

        def blocks(n):
            if n < 4:
                k, q = n // 2, n % 2
                return ([fc_in[:, 4 * q + m, k * P:(k + 1) * P] for m in range(4)],
                        fcT[:, k, q * 512:(q + 1) * 512])
            if n < 8:
                q = n - 4
                return ([proj_in[:, m % 2, (2 * q + m // 2) * P:(2 * q + m // 2 + 1) * P] for m in range(4)],
                        projT[:, 2 * q:2 * q + 2, :].rearrange("p a b -> p (a b)"))
            if n < 10:
                q = n - 8
                return ([u_nat[:, 4 * q + m, :] for m in range(4)], U[:, q * 512:(q + 1) * 512])
            if n < 11:
                return ([W1_in[:, m % 2, (m // 2) * P:(m // 2 + 1) * P] for m in range(4)],
                        W1T[:, :, :].rearrange("p a b -> p (a b)"))
            if n < 13:
                k = n - 11
                return ([Wc_in[:, m % 2, (m // 2) * D + k * P:(m // 2) * D + (k + 1) * P] for m in range(4)],
                        WcT[:, k, :])
            return ([proj_wide[:, m % 2, :] for m in range(4)],
                    proj_row[:, :, :].rearrange("p a b -> p (a b)"))
        BLOCKS = 14
        FC_TERN, PROJ_TERN, U_READY, WIDE_READY = 1, 2, 3, 4
        NEEDS = [FC_TERN] * 4 + [PROJ_TERN] * 4 + [U_READY] * 2 + [0] * 3 + [WIDE_READY]
        LOADS = 13

        def claim(pe, use):
            if use is None:
                return
            if use.name == "up":
                wait(pe, relu_done, use.tile + 1)
            elif use.name == "z":
                wait(pe, zl_done, use.group + 1)
            elif use.name == "hidden":
                wait(pe, tanh_done, use.number + 1)
            else:
                wait(pe, scored, use.number + 1)

        @block.sync
        def _(sp):
            def do(steps, part):
                for s in steps:
                    if s.name == "load":
                        if s.group is not None:
                            wait(sp, added, 2 * (s.group + 1))
                        sp.dma_start(X0[s.half][:, :, :],
                                     x[s.batch.value, s.half * G:(s.half + 1) * G, :]
                                     .rearrange("(c p) d -> p c d", p=P)).then_inc(x_loaded[s.half], 16)
                    elif s.name == "land" and s.kind == "D":
                        wait(sp, added, 2 * (s.group + 1))
                        sp.dma_start(out[s.batch.value, s.half * G:(s.half + 1) * G, :]
                                     .rearrange("(c p) d -> p c d", p=P),
                                     XO[s.half][:, :, :]).then_inc(stored[s.half], 16)
            for counted in counting:
                sp.sem_inc(counted, PRIMED)
            run_parts(sp, do)
            for h in range(2):
                wait(sp, stored[h], Num(16 * B))

        @block.gpsimd
        def _(pool):
            nc.gpsimd.memset(ident[:, :], 0.0).then_inc(pool_prep, 1)
            nc.gpsimd.memset(ones[:, :], 1.0).then_inc(pool_prep, 1)
            nc.gpsimd.memset(exponent[:, :], -0.5).then_inc(pool_prep, 1)
            pool.wait_ge(pool_prep, 3)
            nc.gpsimd.affine_select(out=ident[:, :], in_=ident[:, :], compare_op=ALU.not_equal, fill=1.0,
                                    base=0, pattern=[[-1, P]], channel_multiplier=1).then_inc(const_done, 1)
            nc.gpsimd.affine_select(out=tri_f[:, :], in_=ones[:, :], compare_op=ALU.is_ge, fill=0.0,
                                    base=0, pattern=[[1, P]], channel_multiplier=-1).then_inc(const_done, 1)

            def do(steps, part):
                for s in steps:
                    if s.name == "stats":
                        q = s.prep
                        wait_apart(pool, (const_done, 2), (moments_done, q + 1))
                        nc.gpsimd.tensor_scalar(var_eps[:, :], moments[:, :, 1], EPS, None, ALU.add)\
                            .then_inc(var_done, 1)
                        wait(pool, var_done, q + 1)
                        wait(pool, xn_ready, q)
                        nc.gpsimd.tensor_tensor(rstd[:, :], var_eps[:, :], exponent[:, :], ALU.pow)\
                            .then_inc(rstd_done, 1)
                    elif s.name == "land":
                        g = s.group
                        src, dst = (X0, XA) if s.kind == "A" else (XB, XO)
                        if s.kind == "A":
                            wait(pool, x2_ready, s.mixed)
                        else:
                            wait(pool, stored[s.half], 16 * s.batch)
                        for h in range(2):
                            wait(pool, landed, 2 * g + h + 1)
                            nc.gpsimd.tensor_tensor(dst[s.half][:, 2 * h:2 * h + 2, :],
                                                    src[s.half][:, 2 * h:2 * h + 2, :],
                                                    ffn[h][:, :, :], ALU.add).then_inc(added, 1)
                    elif s.name == "sum":
                        m = s.chunk
                        half, c = s.c // GC, s.c % GC
                        wait(pool, gate_done, m + 1)
                        if c == 0:
                            wait(pool, added, 2 * s.base)
                        nc.gpsimd.tensor_tensor(XB[half][:, c, :], XA[half][:, c, :], th[s.c % 2][:, :],
                                                ALU.add).then_inc(x2_ready, 1)
                    elif s.name == "peak":
                        wait_apart(pool, (const_done, 2), (rowmax_done, s.batch + 1))
                        nc.gpsimd.partition_all_reduce(peak[:, :], row_max[:, :], P, RMAX).then_inc(peak_done, 1)
                        wait_apart(pool, (const_done, 2), (peak_done, s.batch + 1))
                        nc.gpsimd.tensor_scalar(minus_peak[:, :], peak[:, :], -1.0, None, ALU.mult)\
                            .then_inc(minus_peak_done, 1)
            run_parts(pool, do)

        @block.scalar
        def _(act):
            for dst, src in (
                (fc_in[:, :, :], w_fc.rearrange("(t p) d -> p t d", p=P)),
                (proj_in[:, :, :], w_proj.rearrange("(t p) h -> p t h", p=P)),
                (u_in[:, :, :], u.rearrange("(t p) r -> p t r", p=P)),
                (v_in[:, :], v),
                (fbT_in[:, :], fast_b.rearrange("a b -> b a")),
                (gateb[:, :], gate.partition_broadcast(P)),
                (W1_in[:, :, :], W1.rearrange("(t p) d -> p t d", p=P)),
                (Wc_in[:, :, :], Wc.rearrange("(t p) d -> p t d", p=P)),
                (b1c[:, :], b1.rearrange("(n p) -> p n", p=P)),
                (w2c[:, :], w2.rearrange("a (n p) -> p (a n)", p=P)),
                (bcb[:, :], bc.partition_broadcast(P)),
                (b2b[:, :], b2.partition_broadcast(P)),
            ):
                act.dma_start(dst, src, allow_slow_non_contiguous=True).then_inc(w_loaded, 16)
            for n in range(BLOCKS):
                if n % 2 == 0:
                    act.wait_ge(pe_prep, n + 1)
                    nc.scalar.activation(blocks(n)[1], bank[n % 8][:, :], ACT.Copy).then_inc(act_prep, 1)
            act.wait_ge(pe_prep, BLOCKS + 1)
            act.wait_ge(w_loaded, 16 * (LOADS - 1))
            for k in range(KT):
                last = nc.scalar.activation(vf[:, k, :], bank[6][:, k * R:(k + 1) * R], ACT.Copy,
                                            scale=gateb[:, 0:1])
            last.then_inc(act_prep, 1)
            act.wait_ge(act_prep, BLOCKS // 2 + 1)
            nc.scalar.activation(vh[:, :, :], vf[:, :, :], ACT.Copy).then_inc(act_prep, 1)
            act.wait_ge(dve_prep, 5)

            def do(steps, part):
                for s in steps:
                    if s.name == "turn":
                        for k in range(KT):
                            wait(act, turned, 2 * s.prep + k + 1)
                            if s.kind == "B":
                                nc.scalar.activation(xnT[:, k, s.half * G:(s.half + 1) * G],
                                                     turned_bank[k][:, :], ACT.Copy).then_inc(turn_taken, 1)
                            else:
                                nc.scalar.activation(xh[s.group.ring(2)][:, k, :], turned_bank[k][:, :],
                                                     ACT.Copy).then_inc(hi_done, 1)
                    elif s.name == "z":
                        wait(act, z_done, s.group + 1)
                        nc.scalar.activation(zt[s.group.ring(2)][:, :], work[s.bank][:, :], ACT.Copy)\
                            .then_inc(zh_done, 1)
                    elif s.name == "up":
                        t = s.tile
                        wait(act, up_done, t + 1)
                        if t.each or t.first >= 2:
                            wait(act, sq_done, t - 1)
                        nc.scalar.activation(r[t.ring(2)][:, :], work[s.bank][:, :], ACT.Relu,
                                             scale=fc_scale[:, s.j:s.j + 1]).then_inc(relu_done, 1)
                        if t.each or t.first >= 4:
                            wait(act, down_done, 2 * (t - 3))
                        wait(act, relu_done, t + 1)
                        nc.scalar.activation(r2h[t.ring(4)][:, :], r[t.ring(2)][:, :], ACT.Square)\
                            .then_inc(r2h_done, 1)
                    elif s.name == "hidden":
                        wait(act, hid_done, s.number + 1)
                        nc.scalar.activation(hT[:, s.e, :], work[s.bank][:, :], ACT.Tanh,
                                             bias=b1c[:, s.e:s.e + 1]).then_inc(tanh_done, 1)
                    elif s.name == "exp":
                        b = s.batch
                        wait(act, minus_peak_done, b + 1)
                        wait(act, yl_done, CH * b)
                        nc.scalar.activation(e[:, :], s_all[:, :], ACT.Exp, bias=minus_peak[:, 0:1])\
                            .then_inc(exp_done, 1)
                        wait(act, sum_done, CH * b)
                        wait(act, exp_done, b + 1)
                        nc.scalar.activation(yh[:, :, D:D + 1], e[:, :].rearrange("p (c a) -> p c a", a=1),
                                             ACT.Copy).then_inc(eh_done, 1)
                    elif s.name == "mix":
                        wait(act, mix_done, s.chunk + 1)
                        nc.scalar.activation(yh[:, s.c, 0:D], mix_bank[:, 0:D], ACT.Copy,
                                             scale=e[:, s.c:s.c + 1]).then_inc(yh_done, 1)
                    elif s.name == "sum":
                        m = s.chunk
                        wait(act, pre_done, m + 1)
                        wait(act, x2_ready, m - min(s.c, 1))
                        nc.scalar.activation(th[s.c % 2][:, :], pre[s.c % 2][:, :], ACT.Tanh)\
                            .then_inc(gate_done, 1)
            run_parts(act, do)

        @block.vector
        def _(dve):
            chain = [0]

            def then(ins):
                chain[0] += 1
                ins.then_inc(vector_chain, 1)
                dve.wait_ge(vector_chain, chain[0])

            dve.wait_ge(w_loaded, 16 * (LOADS - 1))
            then(nc.vector.tensor_reduce(fc_sum[:, :], fc_in[:, :, :], AX_X, ALU.add, apply_absolute_value=True))
            then(nc.vector.tensor_scalar(fc_scale[:, :], fc_sum[:, :], 1.0 / D, EPS, ALU.mult, ALU.max))
            nc.vector.tensor_scalar(fc_half[:, :], fc_scale[:, :], 0.5, None, ALU.mult)
            nc.vector.tensor_scalar(fc_nhalf[:, :], fc_scale[:, :], -0.5, None, ALU.mult)
            then(nc.vector.reciprocal(fc_inv[:, :], fc_scale[:, :]))
            for t in range(HT):
                part = below[:, (t % 4) * D:(t % 4 + 1) * D]
                then(nc.vector.tensor_scalar(part, fc_in[:, t, :], fc_nhalf[:, t:t + 1], None, ALU.is_lt))
                last = nc.vector.scalar_tensor_tensor(fc_in[:, t, :], fc_in[:, t, :], fc_half[:, t:t + 1], part,
                                                      ALU.is_gt, ALU.subtract)
            last.then_inc(dve_prep, 1)
            dve.wait_ge(const_done, 2)
            then(nc.vector.tensor_reduce(proj_sum[:, :], proj_in[:, :, :], AX_X, ALU.add, apply_absolute_value=True))
            then(nc.vector.tensor_scalar(proj_sum[:, :], proj_sum[:, :], 1.0 / H, EPS, ALU.mult, ALU.max))
            nc.vector.tensor_scalar(proj_half[:, :], proj_sum[:, :], 0.5, None, ALU.mult)
            then(nc.vector.tensor_scalar(proj_nhalf[:, :], proj_sum[:, :], -0.5, None, ALU.mult))
            for t in range(KT):
                then(nc.vector.tensor_scalar(below[:, :], proj_in[:, t, :], proj_nhalf[:, t:t + 1], None, ALU.is_lt))
                then(nc.vector.scalar_tensor_tensor(proj_in[:, t, :], proj_in[:, t, :], proj_half[:, t:t + 1],
                                                    below[:, :], ALU.is_gt, ALU.subtract))
            nc.vector.tensor_copy(tri[:, :], tri_f[:, :]).then_inc(dve_prep, 1)
            for t in range(HT):
                last = nc.vector.tensor_scalar(us[:, t, :], u_in[:, t, :], fc_inv[:, t:t + 1], None, ALU.mult)
            then(last)
            then(nc.vector.tensor_copy(uh[:, :, :], us[:, :, :]))
            then(nc.vector.tensor_tensor(ul[:, :, :], us[:, :, :], uh[:, :, :].bitcast(F32), ALU.subtract))
            for n in range(P // R):
                last = nc.vector.tensor_copy(u_nat[:, :, n * R:(n + 1) * R], (uh, ul)[n % 2][:, :, :].bitcast(F32))
            last.then_inc(dve_prep, 1)
            for t in range(KT):
                last = nc.vector.tensor_scalar(proj_wide[:, t, :], ones[:, :], proj_half[:, t:t + 1], None, ALU.mult)
            last.then_inc(dve_prep, 1)
            nc.vector.tensor_scalar(rest[:, :], tri_f[:, :], -1.0, 1.0, ALU.mult, ALU.add)
            nc.vector.memset(yh[:, :, D + 1:D + 2].bitcast(F32), 0.0)
            nc.vector.memset(yl[:, :, D + 1:D + 2].bitcast(F32), 0.0)
            for n in range(BLOCKS):
                if n % 2 == 1:
                    dve.wait_ge(pe_prep, n + 1)
                    nc.vector.tensor_copy(blocks(n)[1], bank[n % 8][:, :]).then_inc(copy_prep, 1)
            dve.wait_ge(act_prep, BLOCKS // 2 + 2)
            for n in range(P // R):
                if n // 2 % 2 == 0:
                    last = nc.vector.tensor_copy(V[:, :, n * R:(n + 1) * R], vh[:, :, :].bitcast(F32))
                else:
                    last = nc.vector.tensor_tensor(V[:, :, n * R:(n + 1) * R], vf[:, :, :],
                                                   vh[:, :, :].bitcast(F32), ALU.subtract)
            last.then_inc(dve_prep, 1)

            def do(steps, part):
                for s in steps:
                    if s.name == "stats":
                        q, src = s.prep, {"A": X0, "B": XA, "D": XB}[s.kind][s.half]
                        if s.kind == "A":
                            wait(dve, x_loaded[s.half], 16 * (s.batch + 1))
                        elif s.kind == "B":
                            wait(dve, added, 2 * (s.group + 1))
                        else:
                            wait(dve, x2_ready, s.chunks)
                        wait(dve, moments_done, q)
                        for c in range(GC):
                            last = nc.vector.bn_stats(bn[:, c, :], src[:, c, :])
                        last.then_inc(stats_done, 1)
                        wait(dve, xn_ready, q)
                        wait_apart(dve, (const_done, 2), (stats_done, q + 1))
                        for c in range(GC):
                            last = nc.vector.bn_aggr(moments[:, c, :], bn[:, c, :])
                        last.then_inc(moments_done, 1)
                    elif s.name == "norm":
                        q, src = s.prep, {"A": X0, "B": XA, "D": XB}[s.kind][s.half]
                        wait(dve, rstd_done, q + 1)
                        if q.each or q.first >= 2:
                            wait(dve, turned, 2 * (q - 1))
                        for c in range(GC):
                            last = nc.vector.tensor_scalar(xn[q.ring(2)][:, c, :], src[:, c, :],
                                                           moments[:, c, 0:1], rstd[:, c:c + 1],
                                                           ALU.subtract, ALU.mult)
                        last.then_inc(xn_ready, 1)
                    elif s.name == "turn" and s.kind != "B":
                        g = s.group
                        for k in range(KT):
                            wait(dve, hi_done, 2 * g + k + 1)
                            nc.vector.tensor_tensor(xl[g.ring(2)][:, k, :], turned_bank[k][:, :],
                                                    xh[g.ring(2)][:, k, :].bitcast(F32), ALU.subtract)\
                                .then_inc(turn_taken, 1)
                    elif s.name == "z":
                        low = zt[s.group.ring(2)][P // 2:P, :]
                        wait(dve, zh_done, s.group + 1)
                        nc.vector.tensor_tensor(low, work[s.bank][P // 2:P, :], low.bitcast(F32), ALU.subtract)\
                            .then_inc(zl_done, 1)
                    elif s.name == "up":
                        t = s.tile
                        wait(dve, relu_done, t + 1)
                        nc.vector.tensor_tensor(sq[t.ring(2)][:, :], r[t.ring(2)][:, :], r[t.ring(2)][:, :],
                                                ALU.mult).then_inc(sq_done, 1)
                        wait(dve, r2h_done, t + 1)
                        wait(dve, sq_done, t + 1)
                        nc.vector.tensor_tensor(r2l[t.ring(4)][:, :], sq[t.ring(2)][:, :],
                                                r2h[t.ring(4)][:, :].bitcast(F32), ALU.subtract)\
                            .then_inc(r2l_done, 1)
                    elif s.name == "land":
                        g = s.group
                        for h in range(2):
                            wait(dve, down_done, 2 * (HT * g + HT - 1) + h + 1)
                            if g.each or g.first >= 1:
                                wait(dve, added, 2 * g + h - 1)
                            nc.vector.tensor_tensor(ffn[h][:, :, :],
                                                    acc[h][:, :].rearrange("p (c d) -> p c d", c=2),
                                                    proj_row[:, :, :], ALU.mult).then_inc(landed, 1)
                    elif s.name == "score":
                        wait(dve, score_done, s.number + 1)
                        wait(dve, exp_done, s.batch)
                        nc.vector.tensor_scalar(s_all[:, s.half * GC:(s.half + 1) * GC], work[s.bank][:, 0:GC],
                                                b2b[:, 0:1], None, ALU.add).then_inc(scored, 1)
                    elif s.name == "peak":
                        wait(dve, scored, 2 * (s.batch + 1))
                        nc.vector.reduce_max(row_max[:, :], s_all[:, :], AX_X).then_inc(rowmax_done, 1)
                    elif s.name == "exp":
                        wait(dve, eh_done, s.batch + 1)
                        nc.vector.tensor_tensor(yl[:, :, D:D + 1], e[:, :].rearrange("p (c a) -> p c a", a=1),
                                                yh[:, :, D:D + 1].bitcast(F32), ALU.subtract).then_inc(el_done, 1)
                    elif s.name == "mix":
                        m, c = s.chunk, s.c
                        wait(dve, yh_done, m + 1)
                        nc.vector.scalar_tensor_tensor(yl[:, c, 0:D], mix_bank[:, 0:D], e[:, c:c + 1],
                                                       yh[:, c, 0:D].bitcast(F32), ALU.mult, ALU.subtract)\
                            .then_inc(yl_done, 1)
                        nc.vector.tensor_tensor(own[c % 2][:, :], mix_bank[:, D:2 * D], bcb[:, :], ALU.add)\
                            .then_inc(own_done, 1)
                    elif s.name == "sum":
                        m, c = s.chunk, s.c
                        wait(dve, sum_done, m + 1)
                        wait(dve, pre_done, m)
                        nc.vector.reciprocal(rden[:, :], sum_bank[:, D:D + 1]).then_inc(rden_done, 1)
                        wait(dve, gate_done, m - min(c, 1))
                        wait(dve, own_done, m + 1)
                        wait(dve, rden_done, m + 1)
                        nc.vector.scalar_tensor_tensor(pre[c % 2][:, :], sum_bank[:, 0:D], rden[:, 0:1],
                                                       own[c % 2][:, :], ALU.mult, ALU.add).then_inc(pre_done, 1)
            run_parts(dve, do)

        @block.tensor
        def _(pe):
            pe.wait_ge(w_loaded, 16 * (LOADS - 1))
            pe.wait_ge(const_done, 2)
            for n in range(BLOCKS):
                if NEEDS[n]:
                    pe.wait_ge(dve_prep, NEEDS[n])
                if n >= 8:
                    pe.wait_ge(*((act_prep, (n - 8) // 2 + 1) if n % 2 == 0 else (copy_prep, (n - 8) // 2 + 1)))
                for m, src in enumerate(blocks(n)[0]):
                    last = nc.tensor.transpose(bank[n % 8][:, m * P:(m + 1) * P], src, ident[:, :])
                last.then_inc(pe_prep, 1)
            pe.wait_ge(act_prep, BLOCKS // 2)
            pe.wait_ge(copy_prep, BLOCKS // 2)
            for k in range(KT):
                last = nc.tensor.matmul(bank[6][:, k * R:(k + 1) * R], v_in[:, k * P:(k + 1) * P], fbT_in[:, :],
                                        start=(k == 0), stop=True, skip_group_check=True)
            last.then_inc(pe_prep, 1)
            pe.wait_ge(dve_prep, 5)

            def do(steps, part):
                for s in steps:
                    if s.name == "turn":
                        q = s.prep
                        wait(pe, xn_ready, q + 1)
                        wait(pe, turn_taken, 2 * q)
                        for k in range(KT):
                            for c in range(GC):
                                last = nc.tensor.transpose(turned_bank[k][:, c * P:(c + 1) * P],
                                                           xn[q.ring(2)][:, c, k * P:(k + 1) * P], ident[:, :])
                            last.then_inc(turned, 1)
                    elif s.name == "z":
                        n = s.group.ring(2)
                        wait(pe, turn_taken, 2 * (s.prep + 1))
                        claim(pe, s.before)
                        for k in range(KT):
                            for x_half in (xh, xl):
                                last = nc.tensor.matmul(work[s.bank][:, :], V[:, k, :], x_half[n][:, k, :],
                                                        start=(k == 0 and x_half is xh),
                                                        stop=(k == KT - 1 and x_half is xl))
                        last.then_inc(z_done, 1)
                    elif s.name == "up":
                        n = s.group.ring(2)
                        cols = slice(s.j * P, (s.j + 1) * P)
                        claim(pe, s.before)
                        for k in range(KT):
                            for x_half in (xh, xl):
                                nc.tensor.matmul(work[s.bank][:, :], fcT[:, k, cols], x_half[n][:, k, :],
                                                 start=(k == 0 and x_half is xh), stop=False)
                        if s.j == 0:
                            wait(pe, zl_done, s.group + 1)
                        nc.tensor.matmul(work[s.bank][:, :], U[:, cols], zt[n][:, :], start=False, stop=True)\
                            .then_inc(up_done, 1)
                    elif s.name == "down":
                        t, g = s.tile, s.group
                        wait(pe, r2l_done, t + 1)
                        if s.j == 0:
                            wait(pe, landed, 2 * g)
                        for c in range(GC):
                            for half in (r2h, r2l):
                                last = nc.tensor.matmul(acc[c // 2][:, (c % 2) * D:(c % 2 + 1) * D],
                                                        half[t.ring(4)][:, c * P:(c + 1) * P], projT[:, s.j, :],
                                                        start=(s.j == 0 and c % 2 == 0 and half is r2h),
                                                        stop=(s.j == HT - 1 and half is r2l),
                                                        skip_group_check=True)
                            if c % 2 == 1:
                                last.then_inc(down_done, 1)
                    elif s.name == "hidden":
                        wait(pe, turn_taken, 2 * (s.prep + 1))
                        claim(pe, s.before)
                        for k in range(KT):
                            last = nc.tensor.matmul(work[s.bank][:, :], W1T[:, k, s.e * P:(s.e + 1) * P],
                                                    xnT[:, k, s.half * G:(s.half + 1) * G],
                                                    start=(k == 0), stop=(k == KT - 1))
                        last.then_inc(hid_done, 1)
                    elif s.name == "score":
                        wait(pe, tanh_done, 2 * (s.number + 1))
                        claim(pe, s.before)
                        for c in range(GC):
                            for k in range(KT):
                                last = nc.tensor.matmul(work[s.bank][:, c:c + 1], hT[:, k, c * P:(c + 1) * P],
                                                        w2c[:, k:k + 1], start=(c == 0 and k == 0),
                                                        stop=(k == KT - 1), skip_group_check=True)
                        last.then_inc(score_done, 1)
                    elif s.name == "mix":
                        wait(pe, own_done, s.chunk)
                        for k in range(KT):
                            last = nc.tensor.matmul(mix_bank[:, :], xnT[:, k, s.c * P:(s.c + 1) * P], WcT[:, k, :],
                                                    start=(k == 0), stop=(k == KT - 1))
                        last.then_inc(mix_done, 1)
                    elif s.name == "sum":
                        wait(pe, yl_done, s.chunk + 1)
                        if s.c == 0:
                            wait(pe, el_done, s.batch + 1)
                            wait(pe, pre_done, s.chunk)
                        for half in (yh, yl):
                            last = nc.tensor.matmul(sum_bank[:, 0:NY], tri[:, :], half[:, s.c, :],
                                                    start=(s.c == 0 and half is yh), stop=(half is yl),
                                                    skip_group_check=True)
                        last.then_inc(sum_done, 1)
                    elif s.name == "carry":
                        wait(pe, pre_done, s.chunk + 1)
                        for half in (yh, yl):
                            nc.tensor.matmul(sum_bank[:, 0:NY], rest[:, :], half[:, s.c, :], start=False,
                                             stop=(half is yl), skip_group_check=True)
            run_parts(pe, do)
_INS = ['L0_attn_x', 'L0_attn_W1', 'L0_attn_b1', 'L0_attn_w2', 'L0_attn_b2', 'L0_attn_Wc', 'L0_attn_bc',
        'L0_ffn_fast_b', 'L0_ffn_w_fc', 'L0_ffn_w_proj', 'L0_ffn_u', 'L0_ffn_v', 'L0_ffn_gate']


def kernel(**inputs):
    import numpy as _np
    import concourse.bacc as _bacc
    from concourse import mybir as _mybir
    from concourse.bass_utils import run_bass_kernel_spmd as _run

    nc = _bacc.Bacc("TRN2", target_bir_lowering=False, num_devices=1)
    arrays, args = {}, []
    for name in _INS:
        a = _np.ascontiguousarray(inputs[name])
        if a.ndim == 0:
            a = a.reshape(1)
        arrays[f"in_{name}_dram"] = a
        args.append(nc.dram_tensor(f"in_{name}_dram", a.shape, _mybir.dt.from_np(a.dtype), kind="ExternalInput").ap())
    args.append(nc.dram_tensor("out_0_dram", (B, T, D), _mybir.dt.float32, kind="ExternalOutput").ap())
    macaron(nc, *args)
    r = _run(nc, [arrays], core_ids=[0])
    return r.results[0]["out_0_dram"]
```

```python
from contextlib import ExitStack

import concourse.bass as bass
from concourse import mybir

F32 = mybir.dt.float32
F32R = mybir.dt.float32r
ALU = mybir.AluOpType
ACT = mybir.ActivationFunctionType
AX_X = mybir.AxisListType.X
RMAX = bass.bass_isa.ReduceOp.max

P = 128
B, T, D = 8, 1024, 256
PRIMED = 1
H, R = 1024, 16
KT = D // P
HT = H // P
G = 512
GC = G // P
CH = T // P
EPS = 1e-5
NY = D + 2

LAG = 2


FULL_SLOTS = {
    0: [("stats", "A", 1)],
    1: [("exp", "C", 0), ("mix", "C", 0)],
    2: [("norm", "A", 1)],
    3: [("mix", "C", 1), ("sum", "C", 0), ("carry", "C", 0), ("turn", "A", 1)],
    4: [("sum", "C", 1)],
    5: [("mix", "C", 2), ("carry", "C", 1)],
    6: [("sum", "C", 2), ("mix", "C", 3)],
    7: [("z", "A", 1), ("carry", "C", 2)],
    8: [("sum", "C", 3), ("mix", "C", 4), ("carry", "C", 3)],
    9: [("sum", "C", 4)],
    10: [("mix", "C", 5), ("carry", "C", 4), ("stats", "D", 0)],
    11: [("load", "A", 0), ("sum", "C", 5), ("stats", "B", 0)],
    12: [("mix", "C", 6), ("carry", "C", 5), ("norm", "D", 0)],
    13: [("turn", "D", 0)],
    14: [("sum", "C", 6), ("mix", "C", 7), ("carry", "C", 6), ("norm", "B", 0), ("z", "D", 0)],
    15: [("sum", "C", 7)],
    16: [("stats", "D", 1)],
    17: [("load", "A", 1), ("turn", "B", 0)],
    18: [("hidden", "B", 0, 0), ("norm", "D", 1)],
    20: [("stats", "B", 1), ("hidden", "B", 0, 1), ("turn", "D", 1)],
    21: [("score", "B", 0), ("norm", "B", 1)],
    22: [("z", "D", 1)],
    23: [("turn", "B", 1)],
    25: [("hidden", "B", 1, 0)],
    26: [("stats", "N", 0)],
    27: [("hidden", "B", 1, 1)],
    28: [("norm", "N", 0)],
    30: [("turn", "N", 0)],
    31: [("score", "B", 1), ("peak", "B", 0)],
    32: [("z", "N", 0)],
}

FIRST_SLOTS = {
    -1: [("load", "F", 0), ("load", "F", 1), ("fetch", "A", 0), ("signs", "A", 0), ("stats", "F", 0),
        ("signs", "A", 1), ("weights", "A", 0), ("weights", "A", 1), ("factors", "A", 0), ("norm", "F", 0),
        ("factors", "A", 1), ("weights", "A", 2), ("weights", "A", 3), ("turn", "F", 0), ("weights", "A", 4),
        ("weights", "A", 5), ("signs", "A", 2), ("z", "F", 0)],
    0: [("weights", "A", 6), ("weights", "A", 7), ("weights", "A", 8), ("weights", "A", 9)],
    1: [("stats", "A", 1), ("weights", "A", 10), ("weights", "A", 11)],
    2: [("norm", "A", 1), ("weights", "A", 12), ("weights", "A", 13)],
    3: [("turn", "A", 1)],
    4: [("masks", "A", 0)],
    5: [("z", "A", 1)],
    11: [("load", "A", 0), ("stats", "B", 0)],
    13: [("norm", "B", 0)],
    14: [("turn", "B", 0), ("stats", "N", 0)],
    15: [("norm", "N", 0)],
    16: [("hidden", "B", 0, 0), ("turn", "N", 0)],
    18: [("hidden", "B", 0, 1), ("load", "A", 1)],
    19: [("stats", "B", 1), ("score", "B", 0)],
    20: [("norm", "B", 1)],
    21: [("turn", "B", 1)],
    22: [("hidden", "B", 1, 0), ("hidden", "B", 1, 1)],
    23: [("z", "N", 0)],
    24: [("score", "B", 1), ("peak", "B", 0)],
}

END_SLOTS = {
    0: [("exp", "C", 0), ("mix", "C", 0), ("sum", "C", 0), ("mix", "C", 1), ("carry", "C", 0), ("sum", "C", 1)],
    1: [("mix", "C", 2), ("carry", "C", 1), ("sum", "C", 2)],
    3: [("mix", "C", 3), ("carry", "C", 2), ("sum", "C", 3)],
    4: [("mix", "C", 4), ("carry", "C", 3), ("stats", "D", 0), ("sum", "C", 4), ("norm", "D", 0),
        ("turn", "D", 0)],
    5: [("z", "D", 0), ("mix", "C", 5)],
    6: [("carry", "C", 4)],
    7: [("sum", "C", 5)],
    8: [("mix", "C", 6), ("carry", "C", 5)],
    9: [("sum", "C", 6)],
    10: [("mix", "C", 7), ("carry", "C", 6)],
    11: [("sum", "C", 7), ("stats", "D", 1)],
    12: [("norm", "D", 1)],
    13: [("turn", "D", 1), ("z", "D", 1)],
}

END_D = 6
SLOTS = {"first": FIRST_SLOTS, "full": FULL_SLOTS, "last full": FULL_SLOTS, "end": END_SLOTS}
GROUP_AT = {"first": {0: ("A", 0), HT: ("A", 1)},
            "full": {0: ("A", 0), HT: ("A", 1), 2 * HT: ("D", 0), 3 * HT: ("D", 1)},
            "end": {END_D: ("D", 0), END_D + HT: ("D", 1)}}
GROUP_AT["last full"] = GROUP_AT["full"]


class Num:

    def __init__(self, first, each=0, i=None):
        self.first, self.each, self.i = first, each, i

    def __add__(self, n):
        if isinstance(n, Num):
            return Num(self.first + n.first, self.each + n.each, self.i or n.i)
        return Num(self.first + n, self.each, self.i)

    def __sub__(self, n):
        return self + (-n)

    def __rmul__(self, n):
        return Num(n * self.first, n * self.each, self.i)

    def ring(self, m):
        assert self.each % m == 0
        return self.first % m

    @property
    def value(self):
        return self.first if self.each == 0 else self.first + self.each * self.i


def wait(eng, sem, n):
    if n.each == 0 and n.first <= 0:
        return
    assert n.first >= 0, (sem, n.first)
    eng.wait_ge(sem, (n + PRIMED).value)


def wait_apart(eng, passed, *waits):
    if all(n.each == 0 for _, n in waits):
        for sem, n in waits:
            wait(eng, sem, n)
        return
    values = [eng.to_reg((n + PRIMED).value) for _, n in waits]
    eng.wait_ge(*passed)
    for (sem, _), value in zip(waits, values):
        eng.wait_ge(sem, value)


class Step:

    def __init__(self, name, kind=None, half=None, c=None, j=None, e=None, group=None, tile=None,
                 chunk=None, chunks=None, number=None, batch=None, prep=None, base=None, mixed=None,
                 bank=None, before=None, evens=None):
        self.name, self.kind, self.half = name, kind, half
        self.c, self.j, self.e = c, j, e
        self.group, self.tile = group, tile
        self.evens = evens
        self.chunk, self.chunks = chunk, chunks
        self.number = number
        self.batch, self.prep = batch, prep
        self.base, self.mixed = base, mixed
        self.bank, self.before = bank, before


def steps_of(part, before, i=None, each=None):
    at = {k: Num(v, (each or {}).get(k, 0), i) for k, v in before.items()}
    out = []
    turn_of = {}

    def take(kind, n=1):
        now = at[kind]
        at[kind] = now + n
        return now

    def group_of(phase, half):
        if phase == "N":
            return at["batch group"] + per_batch
        return at["batch group"] + (half if phase == "A" or part == "end" else 2 + half)

    per_batch = len(GROUP_AT[part])

    last_uses = [Step("up", tile=HT * at["batch group"] - 1), Step("score", number=2 * at["a batch"] - 1)]
    if part != "end":
        last_uses.append(Step("z", group=at["batch group"]))
    uses = [[], []] if part == "first" else [last_uses, last_uses]

    def on_bank(step):
        step.bank, step.before = take("item").ring(2), uses[-2]
        uses.append([step])
        return step

    tiles = {s0 + j: (*about, j) for s0, about in GROUP_AT[part].items() for j in range(HT)}
    for s in range(min(SLOTS[part]), max(max(SLOTS[part]), max(tiles) + LAG) + 1):
        todo = SLOTS[part].get(s, [])
        square = None
        if s in tiles:
            phase, half, j = tiles[s]
            g = group_of(phase, half)
            out.append(on_bank(Step("up", group=g, tile=HT * g + j, j=j, evens=HT // 2 * g + j // 2)))
            square = Step("square", tile=HT * g + j, j=j, evens=HT // 2 * g + j // 2)
            todo = [t for t in todo if t[0] == "sum"] + [None] + [t for t in todo if t[0] != "sum"]
        for asked in todo:
            if asked is None:
                out.append(square)
                continue
            name, phase, *rest = asked
            if phase == "N" and part == "last full":
                continue
            half = rest[0]
            kind = "A" if phase in "NF" else phase
            if name == "load":
                if part != "last full":
                    batch = at["a batch"] if phase == "F" else at["a batch"] + 1
                    g = None if phase == "F" else group_of("A", half)
                    out.append(Step("load", half=half, batch=batch, group=g))
            elif name in ("weights", "signs", "factors", "masks", "fetch"):
                out.append(Step(name, number=rest[0]))
            elif name == "norm":
                out.append(Step("norm", kind=kind, half=half, prep=take("norm")))
            elif name == "stats":
                src = {"A": at["a batch"] + (1 if phase == "N" else 0), "B": None, "D": None}[kind]
                out.append(Step("stats", kind=kind, half=half, prep=take("prep"), batch=src,
                                group=group_of("A", half) if kind == "B" else None,
                                chunks=CH * at["c batch"] + GC * (half + 1)))
            elif name == "turn":
                q = take("turn")
                turn_of[phase, half] = q
                g = None if kind == "B" else (Num(0) if phase == "F" else group_of(phase, half))
                out.append(Step("turn", kind=kind, half=half, prep=q, group=g))
            elif name == "z":
                g = Num(0) if phase == "F" else group_of(phase, half)
                out.append(on_bank(Step("z", group=g, prep=turn_of[phase, half])))
            elif name == "hidden":
                e = rest[1]
                out.append(on_bank(Step("hidden", half=half, e=e, number=2 * (2 * at["a batch"] + half) + e,
                                        prep=turn_of["B", half])))
            elif name == "score":
                out.append(on_bank(Step("score", half=half, number=2 * at["a batch"] + half,
                                        batch=at["a batch"])))
            elif name == "peak":
                out.append(Step("peak", batch=at["a batch"]))
            elif name == "exp":
                out.append(Step("exp", batch=at["c batch"]))
            else:
                c = rest[0]
                out.append(Step(name, c=c, chunk=CH * at["c batch"] + c, batch=at["c batch"],
                                base=at["batch group"]))
        if s - LAG in tiles:
            phase, half, j = tiles[s - LAG]
            g = group_of(phase, half)
            out.append(Step("down", group=g, tile=HT * g + j, j=j))
            if j == HT - 1:
                out.append(Step("land", kind=phase, half=half, group=g, batch=at["c batch"],
                                mixed=Num(0) if part == "first" else CH * at["c batch"] + GC * (half + 1)))
    at["batch group"] += per_batch
    at["a batch"] += 1
    if part != "first":
        at["c batch"] += 1
    return out, {k: v.first for k, v in at.items()}


ZERO = {"item": 0, "prep": 0, "norm": 0, "turn": 0, "batch group": 0, "a batch": 0, "c batch": 0}
FULL_TURNS = B - 2


def program_parts():
    _, after_first = steps_of("first", ZERO)
    _, after_one = steps_of("full", after_first)
    each = {k: after_one[k] - after_first[k] for k in after_one}
    after_loop = {k: after_first[k] + FULL_TURNS * each[k] for k in each}
    _, after_last = steps_of("last full", after_loop)
    return [("first", ZERO), ("full", after_first), ("last full", after_loop), ("end", after_last)], each


def run_parts(eng, do):
    parts, each = program_parts()
    for part, before in parts:
        if part == "full":
            with eng.Fori(0, FULL_TURNS) as i:
                do(steps_of(part, before, i, each)[0], part)
        else:
            do(steps_of(part, before)[0], part)


def macaron(nc, x, W1, b1, w2, b2, Wc, bc, fast_b, w_fc, w_proj, u, v, gate, out):
    ctx = ExitStack()
    with ctx:
        def sb(name, shape, dt=F32):
            return ctx.enter_context(nc.sbuf_tensor(name, shape, dt))

        def sem(name):
            return ctx.enter_context(nc.semaphore(name))

        counting = []

        def count(name):
            counting.append(sem(name))
            return counting[-1]

        fcT = sb("fcT", [P, KT, H], F32R)
        projT = sb("projT", [P, HT, D], F32R)
        U = sb("U", [P, H], F32R)
        V = sb("V", [P, KT, P], F32R)
        W1h = sb("W1h", [P, KT, D], F32R)
        W1l = sb("W1l", [P, KT, D], F32R)
        Wch = sb("Wch", [P, KT, 2 * D], F32R)
        Wcl = sb("Wcl", [P, KT, 2 * D], F32R)
        fc_scale = sb("fc_scale", [P, HT])
        proj_row = sb("proj_row", [P, 2, D])
        b1c = sb("b1c", [P, KT])
        w2c = sb("w2c", [P, KT])
        bcb = sb("bcb", [P, D])
        b2b = sb("b2b", [P, 1])
        gateb = sb("gateb", [P, 1])
        ident = sb("ident", [P, P])
        ones = sb("ones", [P, P])
        tri_f = sb("tri_f", [P, P])
        tri = sb("tri", [P, P], F32R)
        rest = sb("rest", [P, P], F32R)
        exponent = sb("exponent", [P, GC])

        fc_in = sb("fc_in", [P, HT, D])
        proj_in = sb("proj_in", [P, KT, H])
        W1_in = sb("W1_in", [P, KT, D])
        u_in = sb("u_in", [P, HT, R])
        v_in = sb("v_in", [R, D])
        fbT_in = sb("fbT_in", [R, R])
        fc_sum = sb("fc_sum", [P, HT])
        fc_half = sb("fc_half", [P, HT])
        fc_inv = sb("fc_inv", [P, HT])
        proj_sum = sb("proj_sum", [P, KT])
        proj_half = sb("proj_half", [P, KT])
        proj_wide = sb("proj_wide", [P, KT, P])
        proj_sign = sb("proj_sign", [P, H])
        proj_mag = sb("proj_mag", [P, H])
        us = sb("us", [P, HT, R])
        uh = sb("uh", [P, HT, R], F32R)
        ul = sb("ul", [P, HT, R], F32R)
        u_nat = sb("u_nat", [P, HT, P])
        vf = sb("vf", [P, KT, R])
        vh = sb("vh", [P, KT, R], F32R)

        X0 = [sb(f"X0_{h}", [P, GC, D]) for h in range(2)]
        XA = [sb(f"XA_{h}", [P, GC, D]) for h in range(2)]
        XB = [sb(f"XB_{h}", [P, GC, D]) for h in range(2)]
        XO = [sb(f"XO_{h}", [P, GC, D]) for h in range(2)]
        bn = sb("bn", [P, GC, 6])
        moments = [sb(f"moments{n}", [P, GC, 2]) for n in range(2)]
        var_eps = [sb(f"var_eps{n}", [P, GC]) for n in range(2)]
        rstd = [sb(f"rstd{n}", [P, GC]) for n in range(2)]
        minus_mean = [sb(f"minus_mean{n}", [P, GC]) for n in range(2)]
        shift = [sb(f"shift{n}", [P, GC]) for n in range(2)]
        xn = [sb(f"xn{n}", [P, GC, D]) for n in range(2)]
        xh = [sb(f"xh{n}", [P, KT, G], F32R) for n in range(2)]
        xl = [sb(f"xl{n}", [P, KT, G], F32R) for n in range(2)]
        zt = [sb(f"zt{n}", [P, G], F32R) for n in range(2)]
        r = [sb(f"r{n}", [P, G]) for n in range(2)]
        sq = [sb(f"sq{n}", [P, G]) for n in range(2)]
        r2h = [sb(f"r2h{n}", [P, G], F32R) for n in range(4)]
        r2l = [sb(f"r2l{n}", [P, G], F32R) for n in range(4)]
        ffn = [sb(f"ffn{n}", [P, 2, D]) for n in range(2)]
        xnTh = sb("xnTh", [P, KT, T], F32R)
        xnTl = sb("xnTl", [P, KT, T], F32R)
        hT = sb("hT", [P, KT, G])
        s_all = sb("s_all", [P, CH])
        row_max = sb("row_max", [P, 1])
        peak = sb("peak", [P, 1])
        minus_peak = sb("minus_peak", [P, 1])
        e = sb("e", [P, CH])
        yh = sb("yh", [P, CH, NY], F32R)
        yl = sb("yl", [P, CH, NY], F32R)
        own = [sb(f"own{n}", [P, D]) for n in range(2)]
        rden = sb("rden", [P, 1])
        pre = [sb(f"pre{n}", [P, D]) for n in range(2)]
        th = [sb(f"th{n}", [P, D]) for n in range(2)]

        def flat(a):
            return a.rearrange("p a b -> p (a b)")

        Wc_in = XO[1][:, :, :].rearrange("p (k n) d -> p k (n d)", k=KT)

        fc_abs, fc_sign = (XO[0], XB[0]), (XO[1], XB[1])
        proj_abs, proj_signs = (flat(xn[1][:, :, :]), proj_mag[:, :]), (flat(hT[:, :, :]), proj_sign[:, :])

        bank = [ctx.enter_context(nc.psum_tensor(f"bank{n}", [P, 512], F32)) for n in range(8)]
        work, acc, turned_bank, mix_bank, sum_bank = bank[0:2], bank[2:4], bank[4:6], bank[6], bank[7]

        x_loaded = [count(f"x_loaded{h}") for h in range(2)]
        stored = [count(f"stored{h}") for h in range(2)]
        loaded = {name: sem(f"loaded_{name}") for name in (
            "fc0", "fc1", "u", "v", "fast_b", "gate", "proj", "W1", "Wc", "b1", "w2", "bc", "b2")}
        memset_done, const_done, vector_chain, scalar_chain = (
            sem("memset_done"), sem("const_done"), sem("vector_chain"), sem("scalar_chain"))
        signs_read, signs_done = sem("signs_read"), sem("signs_done")
        u_ready, vf_psum, vf_ready, v_ready = sem("u_ready"), sem("vf_psum"), sem("vf_ready"), sem("v_ready")
        wide_ready, masks_done = sem("wide_ready"), sem("masks_done")
        blocks_done, blocks_copied, lows_copied = sem("blocks_done"), sem("blocks_copied"), sem("lows_copied")
        stats_done, moments_done, var_done, rstd_done, xn_ready = (
            count("stats_done"), count("moments_done"), count("var_done"), count("rstd_done"), count("xn_ready"))
        mean_done, shift_done = count("mean_done"), count("shift_done")
        turned, hi_done, turn_taken = count("turned"), count("hi_done"), count("turn_taken")
        z_done, zh_done, zl_done = count("z_done"), count("zh_done"), count("zl_done")
        up_done, relu_done, r2h_done, sq_done, r2l_done = (
            count("up_done"), count("relu_done"), count("r2h_done"), count("sq_done"), count("r2l_done"))
        act_sq_done = count("act_sq_done")
        down_done, landed, added = count("down_done"), count("landed"), count("added")
        hid_done, tanh_done, score_done, scored = (
            count("hid_done"), count("tanh_done"), count("score_done"), count("scored"))
        rowmax_done, peak_done, minus_peak_done = count("rowmax_done"), count("peak_done"), count("minus_peak_done")
        exp_done, eh_done, el_done = count("exp_done"), count("eh_done"), count("el_done")
        mix_done, yh_done, yl_done, own_done = count("mix_done"), count("yh_done"), count("yl_done"), count("own_done")
        sum_done, rden_done, pre_done, gate_done, x2_ready = (
            count("sum_done"), count("rden_done"), count("pre_done"), count("gate_done"), count("x2_ready"))

        block = ctx.enter_context(nc.Block())

        def blocks(n):
            if n < 4:
                q, k = n // 2, n % 2
                return [fc_in[:, 4 * q + m, k * P:(k + 1) * P] for m in range(4)], fcT[:, k, q * 512:(q + 1) * 512]
            if n < 6:
                q = n - 4
                return [u_nat[:, 4 * q + m, :] for m in range(4)], U[:, q * 512:(q + 1) * 512]
            if n < 10:
                q = n - 6
                return ([proj_in[:, m % 2, (2 * q + m // 2) * P:(2 * q + m // 2 + 1) * P] for m in range(4)],
                        flat(projT[:, 2 * q:2 * q + 2, :]))
            if n < 11:
                return [proj_wide[:, m % 2, :] for m in range(4)], flat(proj_row[:, :, :])
            if n < 12:
                return [W1_in[:, m % 2, (m // 2) * P:(m // 2 + 1) * P] for m in range(4)], flat(W1h[:, :, :])
            k = n - 12
            return ([Wc_in[:, m % 2, (m // 2) * D + k * P:(m // 2) * D + (k + 1) * P] for m in range(4)],
                    Wch[:, k, :])

        LOW_BLOCKS = {11: flat(W1l[:, :, :]), 12: Wcl[:, 0, :], 13: Wcl[:, 1, :]}

        BLOCK_BANK = [0, 1, 2, 3, 6, 7] + [6, 7] * 4
        UP_BLOCKS, DOWN_BLOCKS, ALL_BLOCKS = 6, 10, 14

        def halves(s, k):
            if s.kind == "B":
                cols = slice(s.half * G, (s.half + 1) * G)
                return xnTh[:, k, cols], xnTl[:, k, cols]
            return xh[s.group.ring(2)][:, k, :], xl[s.group.ring(2)][:, k, :]

        def claim(pe, uses):
            for use in uses:
                if use.name == "up":
                    wait(pe, relu_done, use.tile + 1)
                elif use.name == "z":
                    wait(pe, zl_done, use.group + 1)
                elif use.name == "hidden":
                    wait(pe, tanh_done, use.number + 1)
                else:
                    wait(pe, scored, use.number + 1)

        half = HT // 2 * P
        WEIGHTS = {
            "fc0": (fc_in[:, 0:HT // 2, :], w_fc[0:half, :].rearrange("(t p) d -> p t d", p=P)),
            "fc1": (fc_in[:, HT // 2:HT, :], w_fc[half:H, :].rearrange("(t p) d -> p t d", p=P)),
            "proj": (proj_in[:, :, :], w_proj.rearrange("(t p) h -> p t h", p=P)),
            "u": (u_in[:, :, :], u.rearrange("(t p) r -> p t r", p=P)),
            "v": (v_in[:, :], v),
            "fast_b": (fbT_in[:, :], fast_b.rearrange("a b -> b a")),
            "gate": (gateb[:, :], gate.partition_broadcast(P)),
            "W1": (W1_in[:, :, :], W1.rearrange("(t p) d -> p t d", p=P)),
            "Wc": (Wc_in, Wc.rearrange("(t p) d -> p t d", p=P)),
            "b1": (b1c[:, :], b1.rearrange("(n p) -> p n", p=P)),
            "w2": (w2c[:, :], w2.rearrange("a (n p) -> p (a n)", p=P)),
            "bc": (bcb[:, :], bc.partition_broadcast(P)),
            "b2": (b2b[:, :], b2.partition_broadcast(P)),
        }

        def fetch(eng, names):
            for name in names:
                eng.dma_start(*WEIGHTS[name], allow_slow_non_contiguous=True).then_inc(loaded[name], 16)

        @block.sync
        def _(sp):
            def do(steps, part):
                for s in steps:
                    if s.name == "fetch":
                        fetch(sp, ("proj", "W1", "b1", "w2", "bc", "b2"))
                        sp.wait_ge(signs_done, 2)
                        fetch(sp, ("Wc",))
                    elif s.name == "load":
                        if s.group is not None:
                            wait(sp, added, 2 * (s.group + 1))
                        sp.dma_start(X0[s.half][:, :, :],
                                     x[s.batch.value, s.half * G:(s.half + 1) * G, :]
                                     .rearrange("(c p) d -> p c d", p=P)).then_inc(x_loaded[s.half], 16)
                    elif s.name == "land" and s.kind == "D":
                        wait(sp, added, 2 * (s.group + 1))
                        sp.dma_start(out[s.batch.value, s.half * G:(s.half + 1) * G, :]
                                     .rearrange("(c p) d -> p c d", p=P),
                                     XO[s.half][:, :, :]).then_inc(stored[s.half], 16)
            fetch(sp, ("fc0", "fc1"))
            for counted in counting:
                sp.sem_inc(counted, PRIMED)
            run_parts(sp, do)
            for h in range(2):
                wait(sp, stored[h], Num(16 * B))

        @block.gpsimd
        def _(pool):
            nc.gpsimd.memset(ident[:, :], 0.0).then_inc(memset_done, 1)
            nc.gpsimd.memset(ones[:, :], 1.0).then_inc(memset_done, 1)
            nc.gpsimd.memset(exponent[:, :], -0.5).then_inc(memset_done, 1)
            pool.wait_ge(memset_done, 3)
            nc.gpsimd.affine_select(out=ident[:, :], in_=ident[:, :], compare_op=ALU.not_equal, fill=1.0,
                                    base=0, pattern=[[-1, P]], channel_multiplier=1).then_inc(const_done, 1)
            nc.gpsimd.affine_select(out=tri_f[:, :], in_=ones[:, :], compare_op=ALU.is_ge, fill=0.0,
                                    base=0, pattern=[[1, P]], channel_multiplier=-1).then_inc(const_done, 1)

            def do(steps, part):
                for s in steps:
                    if s.name == "stats":
                        q = s.prep
                        wait_apart(pool, (const_done, 2), (moments_done, q + 1))
                        nc.gpsimd.tensor_scalar(var_eps[q.ring(2)][:, :], moments[q.ring(2)][:, :, 1], EPS, None, ALU.add)\
                            .then_inc(var_done, 1)
                        nc.gpsimd.tensor_scalar(minus_mean[q.ring(2)][:, :], moments[q.ring(2)][:, :, 0],
                                                -1.0, None, ALU.mult).then_inc(mean_done, 1)
                        wait(pool, mean_done, q + 1)
                        wait(pool, var_done, q + 1)
                        wait(pool, xn_ready, q - 1)
                        nc.gpsimd.tensor_tensor(rstd[q.ring(2)][:, :], var_eps[q.ring(2)][:, :],
                                                exponent[:, :], ALU.pow).then_inc(rstd_done, 1)
                        wait(pool, rstd_done, q + 1)
                        nc.gpsimd.tensor_tensor(shift[q.ring(2)][:, :], minus_mean[q.ring(2)][:, :],
                                                rstd[q.ring(2)][:, :], ALU.mult).then_inc(shift_done, 1)
                    elif s.name == "land":
                        g = s.group
                        src, dst = (X0, XA) if s.kind == "A" else (XB, XO)
                        if s.kind == "A":
                            wait(pool, x2_ready, s.mixed)
                        else:
                            wait(pool, stored[s.half], 16 * s.batch)
                        for h in range(2):
                            wait(pool, landed, 2 * g + h + 1)
                            nc.gpsimd.tensor_tensor(dst[s.half][:, 2 * h:2 * h + 2, :],
                                                    src[s.half][:, 2 * h:2 * h + 2, :],
                                                    ffn[h][:, :, :], ALU.add).then_inc(added, 1)
                    elif s.name == "sum":
                        m = s.chunk
                        half, c = s.c // GC, s.c % GC
                        wait(pool, gate_done, m + 1)
                        if c == 0:
                            wait(pool, added, 2 * s.base)
                        nc.gpsimd.tensor_tensor(XB[half][:, c, :], XA[half][:, c, :], th[s.c % 2][:, :],
                                                ALU.add).then_inc(x2_ready, 1)
                    elif s.name == "peak":
                        wait_apart(pool, (const_done, 2), (rowmax_done, s.batch + 1))
                        nc.gpsimd.partition_all_reduce(peak[:, :], row_max[:, :], P, RMAX).then_inc(peak_done, 1)
                        wait_apart(pool, (const_done, 2), (peak_done, s.batch + 1))
                        nc.gpsimd.tensor_scalar(minus_peak[:, :], peak[:, :], -1.0, None, ALU.mult)\
                            .then_inc(minus_peak_done, 1)
            run_parts(pool, do)

        @block.scalar
        def _(act):
            fetch(act, ("u", "v", "fast_b", "gate"))

            def do(steps, part):
                for s in steps:
                    if s.name == "signs" and s.number < 2:
                        n = s.number
                        rows = fc_in[:, n * HT // 2:(n + 1) * HT // 2, :]
                        act.wait_ge(loaded[f"fc{n}"], 16)
                        nc.scalar.activation(fc_abs[n][:, :, :], rows, ACT.Abs)
                        nc.scalar.activation(fc_sign[n][:, :, :], rows, ACT.Sign).then_inc(signs_read, 1)
                    elif s.name == "signs":
                        act.wait_ge(loaded["proj"], 16)
                        for t in range(KT):
                            nc.scalar.activation(proj_abs[t], proj_in[:, t, :], ACT.Abs,
                                                 accum_out=proj_sum[:, t:t + 1])
                            last = nc.scalar.activation(proj_signs[t], proj_in[:, t, :], ACT.Sign)
                        last.then_inc(signs_read, 1)
                    elif s.name == "factors" and s.number == 0:
                        act.wait_ge(vf_psum, 1)
                        act.wait_ge(loaded["gate"], 16)
                        nc.scalar.activation(flat(vf[:, :, :]), bank[5][:, 0:KT * R], ACT.Copy,
                                             scale=gateb[:, 0:1]).then_inc(scalar_chain, 1)
                        act.wait_ge(scalar_chain, 1)
                        nc.scalar.activation(vh[:, :, :], vf[:, :, :], ACT.Copy).then_inc(vf_ready, 1)
                    elif s.name == "weights":
                        n = s.number
                        act.wait_ge(blocks_done, n + 1)
                        nc.scalar.activation(blocks(n)[1], bank[BLOCK_BANK[n]][:, :], ACT.Copy)\
                            .then_inc(blocks_copied, 1)
                    elif s.name == "norm":
                        q, src = s.prep, {"A": X0, "B": XA, "D": XB}[s.kind][s.half]
                        wait(act, shift_done, q + 1)
                        if q.each or q.first >= 2:
                            wait(act, turned, 2 * (q - 1))
                        for c in range(GC):
                            last = nc.scalar.activation(xn[q.ring(2)][:, c, :], src[:, c, :], ACT.Identity,
                                                        scale=rstd[q.ring(2)][:, c:c + 1],
                                                        bias=shift[q.ring(2)][:, c:c + 1])
                        last.then_inc(xn_ready, 1)
                    elif s.name == "turn":
                        for k in range(KT):
                            wait(act, turned, 2 * s.prep + k + 1)
                            nc.scalar.activation(halves(s, k)[0], turned_bank[k][:, :], ACT.Copy)\
                                .then_inc(hi_done, 1)
                    elif s.name == "z":
                        wait(act, z_done, s.group + 1)
                        nc.scalar.activation(zt[s.group.ring(2)][:, :], work[s.bank][:, :], ACT.Copy)\
                            .then_inc(zh_done, 1)
                    elif s.name == "up":
                        t = s.tile
                        wait(act, up_done, t + 1)
                        if s.j % 2 == 0 and (t.each or t.first >= 2):
                            wait(act, sq_done, s.evens)
                        nc.scalar.activation(r[t.ring(2)][:, :], work[s.bank][:, :], ACT.Relu,
                                             scale=fc_scale[:, s.j:s.j + 1]).then_inc(relu_done, 1)
                        if t.each or t.first >= 4:
                            wait(act, down_done, 2 * (t - 3))
                        wait(act, relu_done, t + 1)
                        nc.scalar.activation(r2h[t.ring(4)][:, :], r[t.ring(2)][:, :], ACT.Square)\
                            .then_inc(r2h_done, 1)
                        if s.j % 2:
                            wait(act, r2l_done, t - 1)
                            nc.scalar.activation(sq[t.ring(2)][:, :], r[t.ring(2)][:, :], ACT.Square)\
                                .then_inc(act_sq_done, 1)
                    elif s.name == "hidden":
                        wait(act, hid_done, s.number + 1)
                        if part == "first":
                            act.wait_ge(loaded["b1"], 16)
                        nc.scalar.activation(hT[:, s.e, :], work[s.bank][:, :], ACT.Tanh,
                                             bias=b1c[:, s.e:s.e + 1]).then_inc(tanh_done, 1)
                    elif s.name == "exp":
                        b = s.batch
                        wait(act, minus_peak_done, b + 1)
                        wait(act, yl_done, CH * b)
                        nc.scalar.activation(e[:, :], s_all[:, :], ACT.Exp, bias=minus_peak[:, 0:1])\
                            .then_inc(exp_done, 1)
                        wait(act, sum_done, CH * b)
                        wait(act, exp_done, b + 1)
                        nc.scalar.activation(yh[:, :, D:D + 1], e[:, :].rearrange("p (c a) -> p c a", a=1),
                                             ACT.Copy).then_inc(eh_done, 1)
                    elif s.name == "mix":
                        wait(act, mix_done, s.chunk + 1)
                        nc.scalar.activation(yh[:, s.c, 0:D], mix_bank[:, 0:D], ACT.Copy,
                                             scale=e[:, s.c:s.c + 1]).then_inc(yh_done, 1)
                    elif s.name == "sum":
                        m = s.chunk
                        wait(act, pre_done, m + 1)
                        wait(act, x2_ready, m - min(s.c, 1))
                        nc.scalar.activation(th[s.c % 2][:, :], pre[s.c % 2][:, :], ACT.Tanh)\
                            .then_inc(gate_done, 1)
            run_parts(act, do)

        @block.vector
        def _(dve):
            chain = [0]

            def then(ins):
                chain[0] += 1
                ins.then_inc(vector_chain, 1)
                dve.wait_ge(vector_chain, chain[0])

            def do(steps, part):
                for s in steps:
                    if s.name == "signs" and s.number < 2:
                        n = s.number
                        t0, t1 = n * HT // 2, (n + 1) * HT // 2
                        dve.wait_ge(loaded[f"fc{n}"], 16)
                        then(nc.vector.tensor_reduce(fc_sum[:, t0:t1], fc_in[:, t0:t1, :], AX_X, ALU.add,
                                                     apply_absolute_value=True))
                        then(nc.vector.tensor_scalar(fc_scale[:, t0:t1], fc_sum[:, t0:t1], 1.0 / D, EPS,
                                                     ALU.mult, ALU.max))
                        nc.vector.reciprocal(fc_inv[:, t0:t1], fc_scale[:, t0:t1])
                        then(nc.vector.tensor_scalar(fc_half[:, t0:t1], fc_scale[:, t0:t1], 0.5, None, ALU.mult))
                        dve.wait_ge(signs_read, n + 1)
                        for t in range(t0, t1):
                            last = nc.vector.scalar_tensor_tensor(fc_in[:, t, :], fc_abs[n][:, t - t0, :],
                                                                  fc_half[:, t:t + 1], fc_sign[n][:, t - t0, :],
                                                                  ALU.is_gt, ALU.mult)
                        last.then_inc(signs_done, 1)
                    elif s.name == "signs":
                        dve.wait_ge(signs_read, 3)
                        then(nc.vector.tensor_scalar(proj_sum[:, :], proj_sum[:, :], 1.0 / H, EPS,
                                                     ALU.mult, ALU.max))
                        then(nc.vector.tensor_scalar(proj_half[:, :], proj_sum[:, :], 0.5, None, ALU.mult))
                        for t in range(KT):
                            last = nc.vector.scalar_tensor_tensor(proj_in[:, t, :], proj_abs[t],
                                                                  proj_half[:, t:t + 1], proj_signs[t],
                                                                  ALU.is_gt, ALU.mult)
                        last.then_inc(signs_done, 1)
                        dve.wait_ge(const_done, 2)
                        for t in range(KT):
                            last = nc.vector.tensor_scalar(proj_wide[:, t, :], ones[:, :], proj_half[:, t:t + 1],
                                                           None, ALU.mult)
                        last.then_inc(wide_ready, 1)
                    elif s.name == "factors" and s.number == 0:
                        dve.wait_ge(vf_ready, 1)
                        blocks_of = V[:, :, :].rearrange("p k (a t b r) -> p k a t b r", t=2, b=2, r=R)
                        for k in range(KT):
                            def four(a):
                                return a[:, k, :].rearrange("p (a b r) -> p a b r", a=1, b=1)\
                                    .to_broadcast([P, 2, 2, R])
                            nc.vector.tensor_copy(blocks_of[:, k, :, 0, :, :], four(vh).bitcast(F32))
                            last = nc.vector.tensor_tensor(blocks_of[:, k, :, 1, :, :], four(vf),
                                                           four(vh).bitcast(F32), ALU.subtract)
                        last.then_inc(v_ready, 1)
                    elif s.name == "factors":
                        dve.wait_ge(loaded["u"], 16)
                        then(nc.vector.tensor_tensor(us[:, :, :], u_in[:, :, :],
                                                     fc_inv[:, :].rearrange("p (t a) -> p t a", a=1)
                                                     .to_broadcast([P, HT, R]), ALU.mult))
                        then(nc.vector.tensor_copy(uh[:, :, :], us[:, :, :]))
                        then(nc.vector.tensor_tensor(ul[:, :, :], us[:, :, :], uh[:, :, :].bitcast(F32),
                                                     ALU.subtract))
                        pairs = u_nat[:, :, :].rearrange("p t (m two r) -> p t m two r", two=2, r=R)
                        for n, part_of_u in enumerate((uh, ul)):
                            last = nc.vector.tensor_copy(
                                pairs[:, :, :, n, :],
                                part_of_u[:, :, :].rearrange("p t (m r) -> p t m r", m=1)
                                .to_broadcast([P, HT, P // (2 * R), R]).bitcast(F32))
                        last.then_inc(u_ready, 1)
                    elif s.name == "weights" and s.number in LOW_BLOCKS:
                        n = s.number
                        dve.wait_ge(blocks_copied, n + 1)
                        nc.vector.tensor_tensor(LOW_BLOCKS[n], bank[BLOCK_BANK[n]][:, :],
                                                blocks(n)[1].bitcast(F32), ALU.subtract).then_inc(lows_copied, 1)
                    elif s.name == "masks":
                        nc.vector.tensor_copy(tri[:, :], tri_f[:, :])
                        nc.vector.tensor_scalar(rest[:, :], tri_f[:, :], -1.0, 1.0, ALU.mult, ALU.add)
                        nc.vector.memset(yh[:, :, D + 1:D + 2].bitcast(F32), 0.0)
                        nc.vector.memset(yl[:, :, D + 1:D + 2].bitcast(F32), 0.0).then_inc(masks_done, 1)
                        dve.wait_ge(loaded["b2"], 16)
                        dve.wait_ge(loaded["bc"], 16)
                    elif s.name == "stats":
                        q, src = s.prep, {"A": X0, "B": XA, "D": XB}[s.kind][s.half]
                        if s.kind == "A":
                            wait(dve, x_loaded[s.half], 16 * (s.batch + 1))
                        elif s.kind == "B":
                            wait(dve, added, 2 * (s.group + 1))
                        else:
                            wait(dve, x2_ready, s.chunks)
                        wait(dve, moments_done, q)
                        for c in range(GC):
                            last = nc.vector.bn_stats(bn[:, c, :], src[:, c, :])
                        last.then_inc(stats_done, 1)
                        wait(dve, xn_ready, q - 1)
                        wait_apart(dve, (const_done, 2), (stats_done, q + 1))
                        for c in range(GC):
                            last = nc.vector.bn_aggr(moments[q.ring(2)][:, c, :], bn[:, c, :])
                        last.then_inc(moments_done, 1)
                    elif s.name == "turn":
                        for k in range(KT):
                            high, low = halves(s, k)
                            wait(dve, hi_done, 2 * s.prep + k + 1)
                            nc.vector.tensor_tensor(low, turned_bank[k][:, :], high.bitcast(F32), ALU.subtract)\
                                .then_inc(turn_taken, 1)
                    elif s.name == "z":
                        low = zt[s.group.ring(2)][P // 2:P, :]
                        wait(dve, zh_done, s.group + 1)
                        nc.vector.tensor_tensor(low, work[s.bank][P // 2:P, :], low.bitcast(F32), ALU.subtract)\
                            .then_inc(zl_done, 1)
                    elif s.name == "square":
                        t = s.tile
                        if s.j % 2 == 0:
                            wait(dve, relu_done, t + 1)
                            if t.each or t.first >= 2:
                                wait(dve, r2l_done, t - 1)
                            nc.vector.tensor_tensor(sq[0][:, :], r[0][:, :], r[0][:, :],
                                                    ALU.mult).then_inc(sq_done, 1)
                            wait(dve, r2h_done, t + 1)
                            wait(dve, sq_done, s.evens + 1)
                        else:
                            wait(dve, act_sq_done, s.evens + 1)
                        nc.vector.tensor_tensor(r2l[t.ring(4)][:, :], sq[t.ring(2)][:, :],
                                                r2h[t.ring(4)][:, :].bitcast(F32), ALU.subtract)\
                            .then_inc(r2l_done, 1)
                    elif s.name == "land":
                        g = s.group
                        if part == "first":
                            dve.wait_ge(blocks_copied, ALL_BLOCKS)
                        for h in range(2):
                            wait(dve, down_done, 2 * (HT * g + HT - 1) + h + 1)
                            if g.each or g.first >= 1:
                                wait(dve, added, 2 * g + h - 1)
                            nc.vector.tensor_tensor(ffn[h][:, :, :],
                                                    acc[h][:, :].rearrange("p (c d) -> p c d", c=2),
                                                    proj_row[:, :, :], ALU.mult).then_inc(landed, 1)
                    elif s.name == "score":
                        wait(dve, score_done, s.number + 1)
                        wait(dve, exp_done, s.batch)
                        nc.vector.tensor_scalar(s_all[:, s.half * GC:(s.half + 1) * GC], work[s.bank][:, 0:GC],
                                                b2b[:, 0:1], None, ALU.add).then_inc(scored, 1)
                    elif s.name == "peak":
                        wait(dve, scored, 2 * (s.batch + 1))
                        nc.vector.reduce_max(row_max[:, :], s_all[:, :], AX_X).then_inc(rowmax_done, 1)
                    elif s.name == "exp":
                        wait(dve, eh_done, s.batch + 1)
                        nc.vector.tensor_tensor(yl[:, :, D:D + 1], e[:, :].rearrange("p (c a) -> p c a", a=1),
                                                yh[:, :, D:D + 1].bitcast(F32), ALU.subtract).then_inc(el_done, 1)
                    elif s.name == "mix":
                        m, c = s.chunk, s.c
                        wait(dve, yh_done, m + 1)
                        nc.vector.scalar_tensor_tensor(yl[:, c, 0:D], mix_bank[:, 0:D], e[:, c:c + 1],
                                                       yh[:, c, 0:D].bitcast(F32), ALU.mult, ALU.subtract)\
                            .then_inc(yl_done, 1)
                        nc.vector.tensor_tensor(own[c % 2][:, :], mix_bank[:, D:2 * D], bcb[:, :], ALU.add)\
                            .then_inc(own_done, 1)
                    elif s.name == "sum":
                        m, c = s.chunk, s.c
                        wait(dve, sum_done, m + 1)
                        wait(dve, pre_done, m)
                        nc.vector.reciprocal(rden[:, :], sum_bank[:, D:D + 1]).then_inc(rden_done, 1)
                        wait(dve, gate_done, m - min(c, 1))
                        wait(dve, own_done, m + 1)
                        wait(dve, rden_done, m + 1)
                        nc.vector.scalar_tensor_tensor(pre[c % 2][:, :], sum_bank[:, 0:D], rden[:, 0:1],
                                                       own[c % 2][:, :], ALU.mult, ALU.add).then_inc(pre_done, 1)
            run_parts(dve, do)

        @block.tensor
        def _(pe):
            def do(steps, part):
                for s in steps:
                    if s.name == "factors" and s.number == 0:
                        pe.wait_ge(loaded["v"], 16)
                        pe.wait_ge(loaded["fast_b"], 16)
                        for k in range(KT):
                            last = nc.tensor.matmul(bank[5][:, k * R:(k + 1) * R], v_in[:, k * P:(k + 1) * P],
                                                    fbT_in[:, :], start=(k == 0), stop=True,
                                                    skip_group_check=True)
                        last.then_inc(vf_psum, 1)
                    elif s.name == "weights":
                        n = s.number
                        if n == 0:
                            pe.wait_ge(const_done, 2)
                        if n < 4:
                            pe.wait_ge(signs_done, n // 2 + 1)
                        elif n < 6:
                            pe.wait_ge(u_ready, 1)
                        elif n < 10:
                            pe.wait_ge(signs_done, 3)
                        elif n < 11:
                            pe.wait_ge(wide_ready, 1)
                        else:
                            pe.wait_ge(loaded["W1" if n == 11 else "Wc"], 16)
                        if n >= 6:
                            pe.wait_ge(blocks_copied, n - 1)
                        if n - 2 in LOW_BLOCKS:
                            pe.wait_ge(lows_copied, 1)
                        for m, src in enumerate(blocks(n)[0]):
                            last = nc.tensor.transpose(bank[BLOCK_BANK[n]][:, m * P:(m + 1) * P], src, ident[:, :])
                        last.then_inc(blocks_done, 1)
                    elif s.name == "turn":
                        q = s.prep
                        wait(pe, xn_ready, q + 1)
                        wait(pe, turn_taken, 2 * q)
                        for k in range(KT):
                            for c in range(GC):
                                last = nc.tensor.transpose(turned_bank[k][:, c * P:(c + 1) * P],
                                                           xn[q.ring(2)][:, c, k * P:(k + 1) * P], ident[:, :])
                            last.then_inc(turned, 1)
                    elif s.name == "z":
                        n = s.group.ring(2)
                        wait(pe, turn_taken, 2 * (s.prep + 1))
                        if part == "first":
                            pe.wait_ge(v_ready, 1)
                            pe.wait_ge(blocks_copied, UP_BLOCKS)
                        claim(pe, s.before)
                        for k in range(KT):
                            for x_half in (xh, xl):
                                last = nc.tensor.matmul(work[s.bank][:, :], V[:, k, :], x_half[n][:, k, :],
                                                        start=(k == 0 and x_half is xh),
                                                        stop=(k == KT - 1 and x_half is xl))
                        last.then_inc(z_done, 1)
                    elif s.name == "up":
                        n = s.group.ring(2)
                        cols = slice(s.j * P, (s.j + 1) * P)
                        claim(pe, s.before)
                        for k in range(KT):
                            for x_half in (xh, xl):
                                nc.tensor.matmul(work[s.bank][:, :], fcT[:, k, cols], x_half[n][:, k, :],
                                                 start=(k == 0 and x_half is xh), stop=False)
                        if s.j == 0:
                            wait(pe, zl_done, s.group + 1)
                        nc.tensor.matmul(work[s.bank][:, :], U[:, cols], zt[n][:, :], start=False, stop=True)\
                            .then_inc(up_done, 1)
                    elif s.name == "down":
                        t, g = s.tile, s.group
                        wait(pe, r2l_done, t + 1)
                        if part == "first":
                            pe.wait_ge(blocks_copied, DOWN_BLOCKS)
                        if s.j == 0:
                            wait(pe, landed, 2 * g)
                        for c in range(GC):
                            for half in (r2h, r2l):
                                last = nc.tensor.matmul(acc[c // 2][:, (c % 2) * D:(c % 2 + 1) * D],
                                                        half[t.ring(4)][:, c * P:(c + 1) * P], projT[:, s.j, :],
                                                        start=(s.j == 0 and c % 2 == 0 and half is r2h),
                                                        stop=(s.j == HT - 1 and half is r2l),
                                                        skip_group_check=True)
                            if c % 2 == 1:
                                last.then_inc(down_done, 1)
                    elif s.name == "hidden":
                        wait(pe, turn_taken, 2 * (s.prep + 1))
                        if part == "first":
                            pe.wait_ge(blocks_copied, ALL_BLOCKS)
                            pe.wait_ge(lows_copied, len(LOW_BLOCKS))
                            pe.wait_ge(loaded["w2"], 16)
                            pe.wait_ge(masks_done, 1)
                        claim(pe, s.before)
                        cols, rows = slice(s.half * G, (s.half + 1) * G), slice(s.e * P, (s.e + 1) * P)
                        products = [(w, t, k) for k in range(KT) for w, t in ((W1h, xnTh), (W1h, xnTl), (W1l, xnTh))]
                        for w, t, k in products:
                            last = nc.tensor.matmul(work[s.bank][:, :], w[:, k, rows], t[:, k, cols],
                                                    start=((w, t, k) == products[0]),
                                                    stop=((w, t, k) == products[-1]))
                        last.then_inc(hid_done, 1)
                    elif s.name == "score":
                        wait(pe, tanh_done, 2 * (s.number + 1))
                        claim(pe, s.before)
                        for c in range(GC):
                            for k in range(KT):
                                last = nc.tensor.matmul(work[s.bank][:, c:c + 1], hT[:, k, c * P:(c + 1) * P],
                                                        w2c[:, k:k + 1], start=(c == 0 and k == 0),
                                                        stop=(k == KT - 1), skip_group_check=True)
                        last.then_inc(score_done, 1)
                    elif s.name == "mix":
                        wait(pe, own_done, s.chunk)
                        cols = slice(s.c * P, (s.c + 1) * P)
                        products = [(t, w, k) for k in range(KT) for t, w in ((xnTh, Wch), (xnTh, Wcl), (xnTl, Wch))]
                        for t, w, k in products:
                            last = nc.tensor.matmul(mix_bank[:, :], t[:, k, cols], w[:, k, :],
                                                    start=((t, w, k) == products[0]),
                                                    stop=((t, w, k) == products[-1]))
                        last.then_inc(mix_done, 1)
                    elif s.name == "sum":
                        wait(pe, yl_done, s.chunk + 1)
                        if s.c == 0:
                            wait(pe, el_done, s.batch + 1)
                            wait(pe, pre_done, s.chunk)
                        for half in (yh, yl):
                            last = nc.tensor.matmul(sum_bank[:, 0:NY], tri[:, :], half[:, s.c, :],
                                                    start=(s.c == 0 and half is yh), stop=(half is yl),
                                                    skip_group_check=True)
                        last.then_inc(sum_done, 1)
                    elif s.name == "carry":
                        wait(pe, pre_done, s.chunk + 1)
                        for half in (yh, yl):
                            nc.tensor.matmul(sum_bank[:, 0:NY], rest[:, :], half[:, s.c, :], start=False,
                                             stop=(half is yl), skip_group_check=True)
            run_parts(pe, do)
_INS = ['L0_attn_x', 'L0_attn_W1', 'L0_attn_b1', 'L0_attn_w2', 'L0_attn_b2', 'L0_attn_Wc', 'L0_attn_bc',
        'L0_ffn_fast_b', 'L0_ffn_w_fc', 'L0_ffn_w_proj', 'L0_ffn_u', 'L0_ffn_v', 'L0_ffn_gate']


def kernel(**inputs):
    import numpy as _np
    import concourse.bacc as _bacc
    from concourse import mybir as _mybir
    from concourse.bass_utils import run_bass_kernel_spmd as _run

    nc = _bacc.Bacc("TRN2", target_bir_lowering=False, num_devices=1)
    arrays, args = {}, []
    for name in _INS:
        a = _np.ascontiguousarray(inputs[name])
        if a.ndim == 0:
            a = a.reshape(1)
        arrays[f"in_{name}_dram"] = a
        args.append(nc.dram_tensor(f"in_{name}_dram", a.shape, _mybir.dt.from_np(a.dtype), kind="ExternalInput").ap())
    args.append(nc.dram_tensor("out_0_dram", (B, T, D), _mybir.dt.float32, kind="ExternalOutput").ap())
    macaron(nc, *args)
    r = _run(nc, [arrays], core_ids=[0])
    return r.results[0]["out_0_dram"]
```

```python
from contextlib import ExitStack

import concourse.bass as bass
from concourse import mybir

F32 = mybir.dt.float32
F32R = mybir.dt.float32r
ALU = mybir.AluOpType
ACT = mybir.ActivationFunctionType
AX_X = mybir.AxisListType.X
RMAX = bass.bass_isa.ReduceOp.max

P = 128
B, T, D = 8, 1024, 256
PRIMED = 1
H, R = 1024, 16
KT = D // P
HT = H // P
G = 512
GC = G // P
CH = T // P
EPS = 1e-5
NY = D + 2

LAG = 2


SLOTS = {
    "first": {
        -1: [("load", "A", 0, 0), ("signs", "A", 0, 0), ("fetch", "A", 0, 0), ("stats", "A", 0, 0),
            ("signs", "A", 0, 1), ("weights", "A", 0, 0), ("weights", "A", 0, 1), ("factors", "A", 0, 0),
            ("signs", "A", 0, 2), ("norm", "A", 0, 0), ("factors", "A", 0, 1), ("weights", "A", 0, 2),
            ("weights", "A", 0, 3), ("turn", "A", 0, 0), ("weights", "A", 0, 4), ("weights", "A", 0, 5),
            ("z", "A", 0, 0)],
        0: [("fetch", "A", 0, 1), ("weights", "A", 0, 6), ("load", "A", 1, 0), ("load", "A", 0, 1)],
        1: [("weights", "A", 0, 7), ("weights", "A", 0, 8), ("weights", "A", 0, 9)],
        2: [("stats", "A", 0, 1), ("weights", "A", 0, 10)],
        3: [("weights", "A", 0, 11), ("weights", "A", 0, 12), ("norm", "A", 0, 1), ("weights", "A", 0, 13)],
        4: [("load", "A", 1, 1)],
        5: [("turn", "A", 0, 1), ("masks", "A", 0, 0)],
        6: [("z", "A", 0, 1)],
        8: [("stats", "A", 1, 0)],
        10: [("norm", "A", 1, 0)],
        11: [("add", "A", 0, 0), ("load", "A", 2, 0), ("stats", "B", 0, 0)],
        12: [("turn", "A", 1, 0)],
        14: [("z", "A", 1, 0), ("norm", "B", 0, 0)],
        15: [("stats", "A", 1, 1)],
        17: [("turn", "B", 0, 0)],
        19: [("hidden", "B", 0, 0, 0), ("norm", "A", 1, 1)],
        20: [("add", "A", 0, 1), ("hidden", "B", 0, 0, 1), ("load", "A", 2, 1), ("stats", "B", 0, 1)],
        21: [("turn", "A", 1, 1)],
        22: [("score", "B", 0, 0), ("z", "A", 1, 1), ("norm", "B", 0, 1)],
        24: [("turn", "B", 0, 1)],
        25: [("hidden", "B", 0, 1, 0)],
        26: [("hidden", "B", 0, 1, 1)],
        27: [("score", "B", 0, 1), ("peak", "B", 0, 0)],
        29: [("exp", "C", 0, 0), ("mix", "C", 0, 0)],
        30: [("sum", "C", 0, 0), ("mix", "C", 0, 1), ("carry", "C", 0, 0)],
        31: [("sum", "C", 0, 1), ("mix", "C", 0, 2), ("carry", "C", 0, 1)],
        32: [("sum", "C", 0, 2), ("mix", "C", 0, 3), ("carry", "C", 0, 2)],
        33: [("sum", "C", 0, 3), ("add", "A", 1, 0), ("mix", "C", 0, 4), ("carry", "C", 0, 3), ("stats", "D", 0, 0)],
        34: [("mix", "C", 0, 5), ("sum", "C", 0, 4), ("carry", "C", 0, 4), ("norm", "D", 0, 0), ("stats", "B", 1, 0),
            ("sum", "C", 0, 5)],
        35: [("mix", "C", 0, 6), ("carry", "C", 0, 5), ("sum", "C", 0, 6), ("mix", "C", 0, 7), ("carry", "C", 0, 6)],
        36: [("turn", "D", 0, 0), ("sum", "C", 0, 7)],
        37: [("z", "D", 0, 0), ("norm", "B", 1, 0), ("add", "A", 1, 1)],
        38: [("stats", "D", 0, 1)],
        39: [("turn", "B", 1, 0), ("stats", "B", 1, 1)],
        41: [("norm", "D", 0, 1), ("hidden", "B", 1, 0, 0)],
        42: [("turn", "D", 0, 1), ("stats", "A", 2, 0), ("norm", "B", 1, 1), ("hidden", "B", 1, 0, 1)],
        44: [("turn", "B", 1, 1)],
        45: [("z", "D", 0, 1), ("score", "B", 1, 0)],
        46: [("hidden", "B", 1, 1, 0), ("norm", "A", 2, 0)],
        47: [("add", "D", 0, 0), ("hidden", "B", 1, 1, 1)],
        48: [("turn", "A", 2, 0)],
        49: [("score", "B", 1, 1), ("peak", "B", 1, 0), ("z", "A", 2, 0)],
        56: [("add", "D", 0, 1)],
    },
    "full": {
        -1: [("exp", "C", 0, 0), ("stats", "A", 1, 1)],
        1: [("mix", "C", 0, 0)],
        2: [("norm", "A", 1, 1)],
        3: [("mix", "C", 0, 1), ("sum", "C", 0, 0), ("carry", "C", 0, 0), ("turn", "A", 1, 1)],
        4: [("sum", "C", 0, 1)],
        5: [("mix", "C", 0, 2), ("carry", "C", 0, 1)],
        6: [("sum", "C", 0, 2), ("mix", "C", 0, 3), ("z", "A", 1, 1)],
        7: [("carry", "C", 0, 2)],
        8: [("sum", "C", 0, 3), ("mix", "C", 0, 4), ("carry", "C", 0, 3)],
        9: [("sum", "C", 0, 4), ("add", "A", 1, 0)],
        10: [("carry", "C", 0, 4), ("mix", "C", 0, 5), ("stats", "D", 0, 0)],
        11: [("load", "A", 2, 0), ("sum", "C", 0, 5), ("stats", "B", 1, 0)],
        12: [("mix", "C", 0, 6), ("norm", "D", 0, 0), ("carry", "C", 0, 5)],
        13: [("turn", "D", 0, 0)],
        14: [("sum", "C", 0, 6), ("mix", "C", 0, 7), ("norm", "B", 1, 0), ("z", "D", 0, 0), ("carry", "C", 0, 6)],
        15: [("sum", "C", 0, 7)],
        16: [("stats", "D", 0, 1)],
        17: [("load", "A", 2, 1), ("turn", "B", 1, 0), ("add", "A", 1, 1)],
        18: [("hidden", "B", 1, 0, 0), ("norm", "D", 0, 1)],
        20: [("hidden", "B", 1, 0, 1), ("stats", "B", 1, 1), ("turn", "D", 0, 1)],
        21: [("norm", "B", 1, 1), ("score", "B", 1, 0)],
        22: [("z", "D", 0, 1)],
        23: [("turn", "B", 1, 1)],
        26: [("add", "D", 0, 0), ("stats", "A", 2, 0), ("hidden", "B", 1, 1, 0)],
        28: [("hidden", "B", 1, 1, 1), ("norm", "A", 2, 0)],
        30: [("score", "B", 1, 1), ("turn", "A", 2, 0)],
        32: [("peak", "B", 1, 0), ("z", "A", 2, 0)],
        33: [("add", "D", 0, 1)],
    },
    "last": {
        0: [("stats", "A", 1, 1)],
        1: [("exp", "C", 0, 0), ("mix", "C", 0, 0)],
        2: [("norm", "A", 1, 1)],
        3: [("mix", "C", 0, 1), ("sum", "C", 0, 0), ("carry", "C", 0, 0), ("turn", "A", 1, 1)],
        4: [("mix", "C", 0, 2), ("sum", "C", 0, 1)],
        5: [("carry", "C", 0, 1)],
        6: [("sum", "C", 0, 2), ("mix", "C", 0, 3), ("z", "A", 1, 1)],
        7: [("carry", "C", 0, 2)],
        8: [("sum", "C", 0, 3), ("mix", "C", 0, 4), ("carry", "C", 0, 3)],
        9: [("sum", "C", 0, 4)],
        10: [("add", "A", 1, 0), ("mix", "C", 0, 5), ("carry", "C", 0, 4), ("stats", "D", 0, 0)],
        11: [("stats", "B", 1, 0), ("sum", "C", 0, 5)],
        12: [("mix", "C", 0, 6), ("carry", "C", 0, 5), ("norm", "D", 0, 0)],
        13: [("turn", "D", 0, 0)],
        14: [("sum", "C", 0, 6), ("mix", "C", 0, 7), ("carry", "C", 0, 6), ("norm", "B", 1, 0), ("z", "D", 0, 0)],
        15: [("sum", "C", 0, 7)],
        16: [("stats", "D", 0, 1)],
        17: [("turn", "B", 1, 0)],
        18: [("add", "A", 1, 1), ("hidden", "B", 1, 0, 0), ("stats", "B", 1, 1), ("norm", "D", 0, 1)],
        20: [("hidden", "B", 1, 0, 1), ("norm", "B", 1, 1), ("turn", "D", 0, 1)],
        22: [("score", "B", 1, 0), ("z", "D", 0, 1), ("turn", "B", 1, 1)],
        24: [("hidden", "B", 1, 1, 0)],
        25: [("hidden", "B", 1, 1, 1)],
        26: [("score", "B", 1, 1), ("peak", "B", 1, 0), ("add", "D", 0, 0), ("exp", "C", 1, 0), ("mix", "C", 1, 0)],
        28: [("sum", "C", 1, 0), ("mix", "C", 1, 1), ("carry", "C", 1, 0)],
        29: [("sum", "C", 1, 1), ("mix", "C", 1, 2), ("carry", "C", 1, 1)],
        30: [("sum", "C", 1, 2), ("mix", "C", 1, 3), ("carry", "C", 1, 2)],
        31: [("sum", "C", 1, 3), ("mix", "C", 1, 4), ("carry", "C", 1, 3), ("stats", "D", 1, 0)],
        32: [("mix", "C", 1, 5)],
        33: [("norm", "D", 1, 0)],
        34: [("add", "D", 0, 1), ("sum", "C", 1, 4), ("carry", "C", 1, 4)],
        35: [("sum", "C", 1, 5), ("mix", "C", 1, 6), ("carry", "C", 1, 5)],
        36: [("turn", "D", 1, 0), ("z", "D", 1, 0), ("sum", "C", 1, 6), ("mix", "C", 1, 7), ("carry", "C", 1, 6)],
        37: [("stats", "D", 1, 1), ("sum", "C", 1, 7)],
        41: [("norm", "D", 1, 1)],
        43: [("turn", "D", 1, 1)],
        44: [("z", "D", 1, 1)],
        49: [("add", "D", 1, 0)],
        57: [("add", "D", 1, 1)],
    },
}

GROUP_AT = {
    "first": {0: ("A", 0, 0), 8: ("A", 0, 1), 17: ("A", 1, 0), 25: ("A", 1, 1), 38: ("D", 0, 0), 46: ("D", 0, 1)},
    "full": {0: ("A", 1, 0), 8: ("A", 1, 1), 16: ("D", 0, 0), 24: ("D", 0, 1)},
    "last": {0: ("A", 1, 0), 8: ("A", 1, 1), 16: ("D", 0, 0), 24: ("D", 0, 1), 37: ("D", 1, 0), 47: ("D", 1, 1)},
}


class Num:

    def __init__(self, first, each=0, i=None):
        self.first, self.each, self.i = first, each, i

    def __add__(self, n):
        if isinstance(n, Num):
            return Num(self.first + n.first, self.each + n.each, self.i or n.i)
        return Num(self.first + n, self.each, self.i)

    def __sub__(self, n):
        return self + (-n)

    def __rmul__(self, n):
        return Num(n * self.first, n * self.each, self.i)

    def ring(self, m):
        assert self.each % m == 0
        return self.first % m

    @property
    def is_zero(self):
        return self.each == 0 and self.first == 0

    @property
    def value(self):
        return self.first if self.each == 0 else self.first + self.each * self.i


def wait(eng, sem, n):
    if n.each == 0 and n.first <= 0:
        return
    assert n.first >= 0, (sem, n.first)
    eng.wait_ge(sem, (n + PRIMED).value)


def wait_apart(eng, passed, *waits):
    if all(n.each == 0 for _, n in waits):
        for sem, n in waits:
            wait(eng, sem, n)
        return
    values = [eng.to_reg((n + PRIMED).value) for _, n in waits]
    eng.wait_ge(*passed)
    for (sem, _), value in zip(waits, values):
        eng.wait_ge(sem, value)


class Step:

    def __init__(self, name, kind=None, half=None, c=None, j=None, e=None, group=None, tile=None,
                 chunk=None, chunks=None, number=None, batch=None, prep=None,
                 bank=None, before=None, evens=None):
        self.name, self.kind, self.half = name, kind, half
        self.c, self.j, self.e = c, j, e
        self.group, self.tile = group, tile
        self.evens = evens
        self.chunk, self.chunks = chunk, chunks
        self.number = number
        self.batch, self.prep = batch, prep
        self.bank, self.before = bank, before


def steps_of(part, before, i=None, each=None):
    at = {k: Num(v, (each or {}).get(k, 0), i) for k, v in before.items()}
    out = []
    turn_of = {}
    ffns = [about for _, about in sorted(GROUP_AT[part].items())]

    def take(kind, n=1):
        now = at[kind]
        at[kind] = now + n
        return now

    def group_of(phase, ahead, half):
        if (phase, ahead, half) in ffns:
            return at["group"] + ffns.index((phase, ahead, half))
        if phase == "A":
            return at["group"] + len(ffns) + half
        return at["group"] - 2 + half

    last_uses = [Step("up", tile=HT * at["group"] - 1), Step("score", number=at["score"] - 1),
                 Step("z", group=at["group"])]
    uses = [[], []] if part == "first" else [last_uses, last_uses]

    def on_bank(step):
        step.bank, step.before = take("item").ring(2), uses[-2]
        uses.append([step])
        return step

    tiles = {s0 + j: (*about, j) for s0, about in GROUP_AT[part].items() for j in range(HT)}
    slots = SLOTS[part]
    for s in range(min(slots), max(max(slots), max(tiles) + LAG) + 1):
        todo = slots.get(s, [])
        if s in tiles:
            phase, ahead, half, j = tiles[s]
            g = group_of(phase, ahead, half)
            out.append(on_bank(Step("up", group=g, tile=HT * g + j, j=j, evens=HT // 2 * g + j // 2)))
            square = Step("square", tile=HT * g + j, j=j, evens=HT // 2 * g + j // 2)
            todo = [t for t in todo if t[0] == "sum"] + [None] + [t for t in todo if t[0] != "sum"]
        for asked in todo:
            if asked is None:
                out.append(square)
                continue
            name, phase, ahead, *rest = asked
            half = rest[0]
            batch = at["batch"] + ahead
            if name in ("weights", "signs", "factors", "masks", "fetch"):
                out.append(Step(name, number=rest[0]))
            elif name == "load":
                used = ahead - (2 if part == "first" else 1)
                g = None if used < 0 else group_of("A", used, half)
                out.append(Step("load", kind="A", half=half, batch=batch, group=g))
            elif name == "stats":
                out.append(Step("stats", kind=phase, half=half, prep=take("prep"), batch=batch,
                                group=group_of("A", ahead, half) if phase == "B" else None,
                                chunks=CH * batch + GC * (half + 1)))
            elif name == "norm":
                out.append(Step("norm", kind=phase, half=half, prep=take("norm"), batch=batch))
            elif name == "turn":
                turn_of[phase, ahead, half] = q = take("turn")
                g = None if phase == "B" else group_of(phase, ahead, half)
                out.append(Step("turn", kind=phase, half=half, prep=q, group=g))
            elif name == "z":
                out.append(on_bank(Step("z", group=group_of(phase, ahead, half),
                                        prep=turn_of[phase, ahead, half])))
            elif name == "hidden":
                e = rest[1]
                out.append(on_bank(Step("hidden", half=half, e=e, number=2 * (2 * batch + half) + e,
                                        prep=turn_of["B", ahead, half])))
            elif name == "score":
                out.append(on_bank(Step("score", half=half, number=take("score"), batch=batch)))
            elif name in ("peak", "exp"):
                out.append(Step(name, batch=batch))
            elif name == "add":
                out.append(Step("add", kind=phase, half=half, group=group_of(phase, ahead, half), batch=batch,
                                chunks=CH * (batch - 1) + GC * (half + 1)))
            else:
                c = rest[0]
                g = None
                if c % GC == 0 and not (part == "first" and ahead == 0):
                    g = group_of("D", ahead - 1, c // GC)
                out.append(Step(name, c=c, chunk=CH * batch + c, batch=batch, group=g))
        if s - LAG in tiles:
            phase, ahead, half, j = tiles[s - LAG]
            g = group_of(phase, ahead, half)
            out.append(Step("down", group=g, tile=HT * g + j, j=j))
            if j == HT - 1:
                out.append(Step("land", group=g))
    at["group"] += len(ffns)
    at["batch"] += 1
    return out, {k: v.first for k, v in at.items()}


ZERO = {"item": 0, "prep": 0, "norm": 0, "turn": 0, "score": 0, "group": 0, "batch": 0}
LOOP_TURNS = B - 3


def program_parts():
    _, after_first = steps_of("first", ZERO)
    _, after_one = steps_of("full", after_first)
    each = {k: after_one[k] - after_first[k] for k in after_one}
    after_loop = {k: after_first[k] + LOOP_TURNS * each[k] for k in each}
    return [("first", ZERO), ("full", after_first), ("last", after_loop)], each


def run_parts(eng, do):
    parts, each = program_parts()
    for part, before in parts:
        if part == "full":
            with eng.Fori(0, LOOP_TURNS) as i:
                do(steps_of(part, before, i, each)[0], part)
        else:
            do(steps_of(part, before)[0], part)


def macaron(nc, x, W1, b1, w2, b2, Wc, bc, fast_b, w_fc, w_proj, u, v, gate, out):
    ctx = ExitStack()
    with ctx:
        def sb(name, shape, dt=F32):
            return ctx.enter_context(nc.sbuf_tensor(name, shape, dt))

        def sem(name):
            return ctx.enter_context(nc.semaphore(name))

        counting = []

        def count(name):
            counting.append(sem(name))
            return counting[-1]

        fcT = sb("fcT", [P, KT, H], F32R)
        projT = sb("projT", [P, HT, D], F32R)
        U = sb("U", [P, H], F32R)
        V = sb("V", [P, KT, P], F32R)
        W1h = sb("W1h", [P, KT, D], F32R)
        W1l = sb("W1l", [P, KT, D], F32R)
        Wch = sb("Wch", [P, KT, 2 * D], F32R)
        Wcl = sb("Wcl", [P, KT, 2 * D], F32R)
        fc_scale = sb("fc_scale", [P, HT])
        proj_row = sb("proj_row", [P, 2, D])
        b1c = sb("b1c", [P, KT])
        w2c = sb("w2c", [P, KT])
        bcb = sb("bcb", [P, D])
        b2b = sb("b2b", [P, 1])
        gateb = sb("gateb", [P, 1])
        ident = sb("ident", [P, P])
        ones = sb("ones", [P, P])
        tri_f = sb("tri_f", [P, P])
        tri = sb("tri", [P, P], F32R)
        rest = sb("rest", [P, P], F32R)
        exponent = sb("exponent", [P, GC])

        fc_in = sb("fc_in", [P, HT, D])
        proj_in = sb("proj_in", [P, KT, H])
        W1_in = sb("W1_in", [P, KT, D])
        u_in = sb("u_in", [P, HT, R])
        v_in = sb("v_in", [R, D])
        fbT_in = sb("fbT_in", [R, R])
        fc_sum = sb("fc_sum", [P, HT])
        fc_half = sb("fc_half", [P, HT])
        fc_inv = sb("fc_inv", [P, HT])
        proj_sum = sb("proj_sum", [P, KT])
        proj_half = sb("proj_half", [P, KT])
        proj_wide = sb("proj_wide", [P, KT, P])
        proj_sign = sb("proj_sign", [P, H])
        proj_mag = sb("proj_mag", [P, H])
        us = sb("us", [P, HT, R])
        uh = sb("uh", [P, HT, R], F32R)
        ul = sb("ul", [P, HT, R], F32R)
        u_nat = sb("u_nat", [P, HT, P])
        vf = sb("vf", [P, KT, R])
        vh = sb("vh", [P, KT, R], F32R)

        X0 = [sb(f"X0_{h}", [P, GC, D]) for h in range(2)]
        XA = [sb(f"XA_{h}", [P, GC, D]) for h in range(2)]
        XB = [sb(f"XB_{h}", [P, GC, D]) for h in range(2)]
        XO = [sb(f"XO_{h}", [P, GC, D]) for h in range(2)]
        bn = sb("bn", [P, GC, 6])
        moments = [sb(f"moments{n}", [P, GC, 2]) for n in range(2)]
        var_eps = [sb(f"var_eps{n}", [P, GC]) for n in range(2)]
        rstd = [sb(f"rstd{n}", [P, GC]) for n in range(2)]
        minus_mean = [sb(f"minus_mean{n}", [P, GC]) for n in range(2)]
        shift = [sb(f"shift{n}", [P, GC]) for n in range(2)]
        xn = [sb(f"xn{n}", [P, GC, D]) for n in range(2)]
        xh = [sb(f"xh{n}", [P, KT, G], F32R) for n in range(2)]
        xl = [sb(f"xl{n}", [P, KT, G], F32R) for n in range(2)]
        zt = [sb(f"zt{n}", [P, G], F32R) for n in range(2)]
        r = [sb(f"r{n}", [P, G]) for n in range(2)]
        sq = [sb(f"sq{n}", [P, G]) for n in range(2)]
        r2h = [sb(f"r2h{n}", [P, G], F32R) for n in range(4)]
        r2l = [sb(f"r2l{n}", [P, G], F32R) for n in range(4)]
        ffn = [sb(f"ffn{n}", [P, 2, D]) for n in range(2)]
        xnTh = sb("xnTh", [P, KT, T], F32R)
        xnTl = sb("xnTl", [P, KT, T], F32R)
        hT = sb("hT", [P, KT, G])
        s_all = sb("s_all", [P, CH])
        row_max = sb("row_max", [P, 1])
        peak = sb("peak", [P, 1])
        minus_peak = sb("minus_peak", [P, 1])
        e = sb("e", [P, CH])
        yh = sb("yh", [P, CH, NY], F32R)
        yl = sb("yl", [P, CH, NY], F32R)
        own = [sb(f"own{n}", [P, D]) for n in range(2)]
        rden = sb("rden", [P, 1])
        pre = [sb(f"pre{n}", [P, D]) for n in range(2)]
        th = [sb(f"th{n}", [P, D]) for n in range(2)]

        def flat(a):
            return a.rearrange("p a b -> p (a b)")

        Wc_in = XO[1][:, :, :].rearrange("p (k n) d -> p k (n d)", k=KT)

        fc_abs, fc_sign = (XO[0], XB[0]), (XO[1], XB[1])
        proj_abs, proj_signs = (flat(xn[1][:, :, :]), proj_mag[:, :]), (flat(hT[:, :, :]), proj_sign[:, :])

        bank = [ctx.enter_context(nc.psum_tensor(f"bank{n}", [P, 512], F32)) for n in range(8)]
        work, acc, turned_bank, mix_bank, sum_bank = bank[0:2], bank[2:4], bank[4:6], bank[6], bank[7]

        x_loaded = [count(f"x_loaded{h}") for h in range(2)]
        stored = [count(f"stored{h}") for h in range(2)]
        loaded = {name: sem(f"loaded_{name}") for name in (
            "fc0", "fc1", "u", "v", "fast_b", "gate", "proj", "W1", "Wc", "b1", "w2", "bc", "b2")}
        memset_done, const_done, vector_chain, scalar_chain = (
            sem("memset_done"), sem("const_done"), sem("vector_chain"), sem("scalar_chain"))
        signs_read, signs_done = sem("signs_read"), sem("signs_done")
        u_ready, vf_psum, vf_ready, v_ready = sem("u_ready"), sem("vf_psum"), sem("vf_ready"), sem("v_ready")
        wide_ready, masks_done = sem("wide_ready"), sem("masks_done")
        blocks_done, blocks_copied, lows_copied = sem("blocks_done"), sem("blocks_copied"), sem("lows_copied")
        stats_done, moments_done, var_done, rstd_done, xn_ready = (
            count("stats_done"), count("moments_done"), count("var_done"), count("rstd_done"), count("xn_ready"))
        mean_done, shift_done = count("mean_done"), count("shift_done")
        turned, hi_done, turn_taken = count("turned"), count("hi_done"), count("turn_taken")
        z_done, zh_done, zl_done = count("z_done"), count("zh_done"), count("zl_done")
        up_done, relu_done, r2h_done, sq_done, r2l_done = (
            count("up_done"), count("relu_done"), count("r2h_done"), count("sq_done"), count("r2l_done"))
        act_sq_done = count("act_sq_done")
        down_done, landed, added = count("down_done"), count("landed"), count("added")
        hid_done, tanh_done, score_done, scored = (
            count("hid_done"), count("tanh_done"), count("score_done"), count("scored"))
        rowmax_done, peak_done, minus_peak_done = count("rowmax_done"), count("peak_done"), count("minus_peak_done")
        exp_done, eh_done, el_done = count("exp_done"), count("eh_done"), count("el_done")
        mix_done, yh_done, yl_done, own_done = count("mix_done"), count("yh_done"), count("yl_done"), count("own_done")
        sum_done, rden_done, pre_done, gate_done, x2_ready = (
            count("sum_done"), count("rden_done"), count("pre_done"), count("gate_done"), count("x2_ready"))

        block = ctx.enter_context(nc.Block())

        def blocks(n):
            if n < 4:
                q, k = n // 2, n % 2
                return [fc_in[:, 4 * q + m, k * P:(k + 1) * P] for m in range(4)], fcT[:, k, q * 512:(q + 1) * 512]
            if n < 6:
                q = n - 4
                return [u_nat[:, 4 * q + m, :] for m in range(4)], U[:, q * 512:(q + 1) * 512]
            if n < 10:
                q = n - 6
                return ([proj_in[:, m % 2, (2 * q + m // 2) * P:(2 * q + m // 2 + 1) * P] for m in range(4)],
                        flat(projT[:, 2 * q:2 * q + 2, :]))
            if n < 11:
                return [proj_wide[:, m % 2, :] for m in range(4)], flat(proj_row[:, :, :])
            if n < 12:
                return [W1_in[:, m % 2, (m // 2) * P:(m // 2 + 1) * P] for m in range(4)], flat(W1h[:, :, :])
            k = n - 12
            return ([Wc_in[:, m % 2, (m // 2) * D + k * P:(m // 2) * D + (k + 1) * P] for m in range(4)],
                    Wch[:, k, :])

        LOW_BLOCKS = {11: flat(W1l[:, :, :]), 12: Wcl[:, 0, :], 13: Wcl[:, 1, :]}

        BLOCK_BANK = [0, 1, 2, 3, 6, 7] + [6, 7] * 4
        UP_BLOCKS, DOWN_BLOCKS, ALL_BLOCKS = 6, 10, 14

        def tokens(s):
            if s.kind == "A":
                return (XO if s.batch.each == 0 and s.batch.first == 1 else X0)[s.half]
            return (XA if s.kind == "B" else XB)[s.half]

        def halves(s, k):
            if s.kind == "B":
                cols = slice(s.half * G, (s.half + 1) * G)
                return xnTh[:, k, cols], xnTl[:, k, cols]
            return xh[s.group.ring(2)][:, k, :], xl[s.group.ring(2)][:, k, :]

        def claim(pe, uses):
            for use in uses:
                if use.name == "up":
                    wait(pe, relu_done, use.tile + 1)
                elif use.name == "z":
                    wait(pe, zl_done, use.group + 1)
                elif use.name == "hidden":
                    wait(pe, tanh_done, use.number + 1)
                else:
                    wait(pe, scored, use.number + 1)

        half = HT // 2 * P
        WEIGHTS = {
            "fc0": (fc_in[:, 0:HT // 2, :], w_fc[0:half, :].rearrange("(t p) d -> p t d", p=P)),
            "fc1": (fc_in[:, HT // 2:HT, :], w_fc[half:H, :].rearrange("(t p) d -> p t d", p=P)),
            "proj": (proj_in[:, :, :], w_proj.rearrange("(t p) h -> p t h", p=P)),
            "u": (u_in[:, :, :], u.rearrange("(t p) r -> p t r", p=P)),
            "v": (v_in[:, :], v),
            "fast_b": (fbT_in[:, :], fast_b.rearrange("a b -> b a")),
            "gate": (gateb[:, :], gate.partition_broadcast(P)),
            "W1": (W1_in[:, :, :], W1.rearrange("(t p) d -> p t d", p=P)),
            "Wc": (Wc_in, Wc.rearrange("(t p) d -> p t d", p=P)),
            "b1": (b1c[:, :], b1.rearrange("(n p) -> p n", p=P)),
            "w2": (w2c[:, :], w2.rearrange("a (n p) -> p (a n)", p=P)),
            "bc": (bcb[:, :], bc.partition_broadcast(P)),
            "b2": (b2b[:, :], b2.partition_broadcast(P)),
        }

        def fetch(eng, names):
            for name in names:
                eng.dma_start(*WEIGHTS[name], allow_slow_non_contiguous=True).then_inc(loaded[name], 16)

        @block.sync
        def _(sp):
            def do(steps, part):
                for s in steps:
                    if s.name == "fetch" and s.number == 0:
                        fetch(sp, ("u", "v", "fast_b", "gate"))
                    elif s.name == "fetch":
                        fetch(sp, ("proj", "W1", "b1", "w2", "bc", "b2"))
                        sp.wait_ge(signs_done, 2)
                        fetch(sp, ("Wc",))
                    elif s.name == "load":
                        if s.group is not None:
                            wait(sp, added, 2 * (s.group + 1))
                        elif s.batch.first == 1 and s.half == 1:
                            sp.wait_ge(blocks_copied, ALL_BLOCKS)
                        elif s.batch.first == 1:
                            sp.wait_ge(signs_done, 1)
                        sp.dma_start(tokens(s)[:, :, :],
                                     x[s.batch.value, s.half * G:(s.half + 1) * G, :]
                                     .rearrange("(c p) d -> p c d", p=P)).then_inc(x_loaded[s.half], 16)
                    elif s.name == "add" and s.kind == "D":
                        wait(sp, added, 2 * (s.group + 1))
                        sp.dma_start(out[s.batch.value, s.half * G:(s.half + 1) * G, :]
                                     .rearrange("(c p) d -> p c d", p=P),
                                     XO[s.half][:, :, :]).then_inc(stored[s.half], 16)
            fetch(sp, ("fc0",))
            run_parts(sp, do)
            for h in range(2):
                wait(sp, stored[h], Num(16 * B))

        @block.gpsimd
        def _(pool):
            nc.gpsimd.memset(ident[:, :], 0.0).then_inc(memset_done, 1)
            nc.gpsimd.memset(ones[:, :], 1.0).then_inc(memset_done, 1)
            nc.gpsimd.memset(exponent[:, :], -0.5).then_inc(memset_done, 1)
            pool.wait_ge(memset_done, 3)
            nc.gpsimd.affine_select(out=ident[:, :], in_=ident[:, :], compare_op=ALU.not_equal, fill=1.0,
                                    base=0, pattern=[[-1, P]], channel_multiplier=1).then_inc(const_done, 1)
            nc.gpsimd.affine_select(out=tri_f[:, :], in_=ones[:, :], compare_op=ALU.is_ge, fill=0.0,
                                    base=0, pattern=[[1, P]], channel_multiplier=-1).then_inc(const_done, 1)
            for counted in counting:
                pool.sem_inc(counted, PRIMED)

            def do(steps, part):
                for s in steps:
                    if s.name == "stats":
                        q = s.prep
                        wait_apart(pool, (const_done, 2), (moments_done, q + 1))
                        nc.gpsimd.tensor_scalar(var_eps[q.ring(2)][:, :], moments[q.ring(2)][:, :, 1], EPS, None, ALU.add)\
                            .then_inc(var_done, 1)
                        nc.gpsimd.tensor_scalar(minus_mean[q.ring(2)][:, :], moments[q.ring(2)][:, :, 0],
                                                -1.0, None, ALU.mult).then_inc(mean_done, 1)
                        wait(pool, mean_done, q + 1)
                        wait(pool, var_done, q + 1)
                        wait(pool, xn_ready, q - 1)
                        nc.gpsimd.tensor_tensor(rstd[q.ring(2)][:, :], var_eps[q.ring(2)][:, :],
                                                exponent[:, :], ALU.pow).then_inc(rstd_done, 1)
                        wait(pool, rstd_done, q + 1)
                        nc.gpsimd.tensor_tensor(shift[q.ring(2)][:, :], minus_mean[q.ring(2)][:, :],
                                                rstd[q.ring(2)][:, :], ALU.mult).then_inc(shift_done, 1)
                    elif s.name == "add":
                        g = s.group
                        src, dst = tokens(s), (XA if s.kind == "A" else XO)[s.half]
                        if s.kind == "A":
                            wait(pool, x2_ready, s.chunks)
                        else:
                            wait(pool, stored[s.half], 16 * s.batch)
                            wait(pool, added, 2 * g)
                        for h in range(2):
                            wait(pool, landed, 2 * g + h + 1)
                            nc.gpsimd.tensor_tensor(dst[:, 2 * h:2 * h + 2, :], src[:, 2 * h:2 * h + 2, :],
                                                    ffn[h][:, :, :], ALU.add).then_inc(added, 1)
                    elif s.name == "sum":
                        m = s.chunk
                        half, c = s.c // GC, s.c % GC
                        wait(pool, gate_done, m + 1)
                        if s.group is not None:
                            wait(pool, added, 2 * (s.group + 1))
                        nc.gpsimd.tensor_tensor(XB[half][:, c, :], XA[half][:, c, :], th[s.c % 2][:, :],
                                                ALU.add).then_inc(x2_ready, 1)
                    elif s.name == "peak":
                        wait_apart(pool, (const_done, 2), (rowmax_done, s.batch + 1))
                        nc.gpsimd.partition_all_reduce(peak[:, :], row_max[:, :], P, RMAX).then_inc(peak_done, 1)
                        wait_apart(pool, (const_done, 2), (peak_done, s.batch + 1))
                        nc.gpsimd.tensor_scalar(minus_peak[:, :], peak[:, :], -1.0, None, ALU.mult)\
                            .then_inc(minus_peak_done, 1)
            run_parts(pool, do)

        @block.scalar
        def _(act):
            fetch(act, ("fc1",))

            def do(steps, part):
                for s in steps:
                    if s.name == "signs" and s.number < 2:
                        n = s.number
                        rows = fc_in[:, n * HT // 2:(n + 1) * HT // 2, :]
                        act.wait_ge(loaded[f"fc{n}"], 16)
                        nc.scalar.activation(fc_abs[n][:, :, :], rows, ACT.Abs)
                        nc.scalar.activation(fc_sign[n][:, :, :], rows, ACT.Sign).then_inc(signs_read, 1)
                    elif s.name == "signs":
                        act.wait_ge(loaded["proj"], 16)
                        for t in range(KT):
                            nc.scalar.activation(proj_abs[t], proj_in[:, t, :], ACT.Abs,
                                                 accum_out=proj_sum[:, t:t + 1])
                            last = nc.scalar.activation(proj_signs[t], proj_in[:, t, :], ACT.Sign)
                        last.then_inc(signs_read, 1)
                    elif s.name == "factors" and s.number == 0:
                        act.wait_ge(vf_psum, 1)
                        act.wait_ge(loaded["gate"], 16)
                        nc.scalar.activation(flat(vf[:, :, :]), bank[5][:, 0:KT * R], ACT.Copy,
                                             scale=gateb[:, 0:1]).then_inc(scalar_chain, 1)
                        act.wait_ge(scalar_chain, 1)
                        nc.scalar.activation(vh[:, :, :], vf[:, :, :], ACT.Copy).then_inc(vf_ready, 1)
                    elif s.name == "weights":
                        n = s.number
                        act.wait_ge(blocks_done, n + 1)
                        nc.scalar.activation(blocks(n)[1], bank[BLOCK_BANK[n]][:, :], ACT.Copy)\
                            .then_inc(blocks_copied, 1)
                    elif s.name == "norm":
                        q, src = s.prep, tokens(s)
                        wait(act, shift_done, q + 1)
                        if q.each or q.first >= 2:
                            wait(act, turned, 2 * (q - 1))
                        for c in range(GC):
                            last = nc.scalar.activation(xn[q.ring(2)][:, c, :], src[:, c, :], ACT.Identity,
                                                        scale=rstd[q.ring(2)][:, c:c + 1],
                                                        bias=shift[q.ring(2)][:, c:c + 1])
                        last.then_inc(xn_ready, 1)
                    elif s.name == "turn":
                        for k in range(KT):
                            wait(act, turned, 2 * s.prep + k + 1)
                            nc.scalar.activation(halves(s, k)[0], turned_bank[k][:, :], ACT.Copy)\
                                .then_inc(hi_done, 1)
                    elif s.name == "z":
                        wait(act, z_done, s.group + 1)
                        nc.scalar.activation(zt[s.group.ring(2)][:, :], work[s.bank][:, :], ACT.Copy)\
                            .then_inc(zh_done, 1)
                    elif s.name == "up":
                        t = s.tile
                        wait(act, up_done, t + 1)
                        if s.j % 2 == 0 and (t.each or t.first >= 2):
                            wait(act, sq_done, s.evens)
                        nc.scalar.activation(r[t.ring(2)][:, :], work[s.bank][:, :], ACT.Relu,
                                             scale=fc_scale[:, s.j:s.j + 1]).then_inc(relu_done, 1)
                        if t.each or t.first >= 4:
                            wait(act, down_done, 2 * (t - 3))
                        wait(act, relu_done, t + 1)
                        nc.scalar.activation(r2h[t.ring(4)][:, :], r[t.ring(2)][:, :], ACT.Square)\
                            .then_inc(r2h_done, 1)
                        if s.j % 2:
                            wait(act, r2l_done, t - 1)
                            nc.scalar.activation(sq[t.ring(2)][:, :], r[t.ring(2)][:, :], ACT.Square)\
                                .then_inc(act_sq_done, 1)
                    elif s.name == "hidden":
                        wait(act, hid_done, s.number + 1)
                        if s.number.is_zero:
                            act.wait_ge(loaded["b1"], 16)
                        nc.scalar.activation(hT[:, s.e, :], work[s.bank][:, :], ACT.Tanh,
                                             bias=b1c[:, s.e:s.e + 1]).then_inc(tanh_done, 1)
                    elif s.name == "exp":
                        b = s.batch
                        wait(act, minus_peak_done, b + 1)
                        wait(act, yl_done, CH * b)
                        nc.scalar.activation(e[:, :], s_all[:, :], ACT.Exp, bias=minus_peak[:, 0:1])\
                            .then_inc(exp_done, 1)
                        wait(act, sum_done, CH * b)
                        wait(act, exp_done, b + 1)
                        nc.scalar.activation(yh[:, :, D:D + 1], e[:, :].rearrange("p (c a) -> p c a", a=1),
                                             ACT.Copy).then_inc(eh_done, 1)
                    elif s.name == "mix":
                        wait(act, mix_done, s.chunk + 1)
                        nc.scalar.activation(yh[:, s.c, 0:D], mix_bank[:, 0:D], ACT.Copy,
                                             scale=e[:, s.c:s.c + 1]).then_inc(yh_done, 1)
                    elif s.name == "sum":
                        m = s.chunk
                        wait(act, pre_done, m + 1)
                        wait(act, x2_ready, m - 1)
                        nc.scalar.activation(th[s.c % 2][:, :], pre[s.c % 2][:, :], ACT.Tanh)\
                            .then_inc(gate_done, 1)
            run_parts(act, do)

        @block.vector
        def _(dve):
            chain = [0]

            def then(ins):
                chain[0] += 1
                ins.then_inc(vector_chain, 1)
                dve.wait_ge(vector_chain, chain[0])

            def do(steps, part):
                for s in steps:
                    if s.name == "signs" and s.number < 2:
                        n = s.number
                        t0, t1 = n * HT // 2, (n + 1) * HT // 2
                        dve.wait_ge(loaded[f"fc{n}"], 16)
                        then(nc.vector.tensor_reduce(fc_sum[:, t0:t1], fc_in[:, t0:t1, :], AX_X, ALU.add,
                                                     apply_absolute_value=True))
                        then(nc.vector.tensor_scalar(fc_scale[:, t0:t1], fc_sum[:, t0:t1], 1.0 / D, EPS,
                                                     ALU.mult, ALU.max))
                        nc.vector.reciprocal(fc_inv[:, t0:t1], fc_scale[:, t0:t1])
                        then(nc.vector.tensor_scalar(fc_half[:, t0:t1], fc_scale[:, t0:t1], 0.5, None, ALU.mult))
                        dve.wait_ge(signs_read, n + 1)
                        for t in range(t0, t1):
                            last = nc.vector.scalar_tensor_tensor(fc_in[:, t, :], fc_abs[n][:, t - t0, :],
                                                                  fc_half[:, t:t + 1], fc_sign[n][:, t - t0, :],
                                                                  ALU.is_gt, ALU.mult)
                        last.then_inc(signs_done, 1)
                    elif s.name == "signs":
                        dve.wait_ge(signs_read, 3)
                        then(nc.vector.tensor_scalar(proj_sum[:, :], proj_sum[:, :], 1.0 / H, EPS,
                                                     ALU.mult, ALU.max))
                        then(nc.vector.tensor_scalar(proj_half[:, :], proj_sum[:, :], 0.5, None, ALU.mult))
                        for t in range(KT):
                            last = nc.vector.scalar_tensor_tensor(proj_in[:, t, :], proj_abs[t],
                                                                  proj_half[:, t:t + 1], proj_signs[t],
                                                                  ALU.is_gt, ALU.mult)
                        last.then_inc(signs_done, 1)
                        dve.wait_ge(const_done, 2)
                        for t in range(KT):
                            last = nc.vector.tensor_scalar(proj_wide[:, t, :], ones[:, :], proj_half[:, t:t + 1],
                                                           None, ALU.mult)
                        last.then_inc(wide_ready, 1)
                    elif s.name == "factors" and s.number == 0:
                        dve.wait_ge(vf_ready, 1)
                        blocks_of = V[:, :, :].rearrange("p k (a t b r) -> p k a t b r", t=2, b=2, r=R)
                        for k in range(KT):
                            def four(a):
                                return a[:, k, :].rearrange("p (a b r) -> p a b r", a=1, b=1)\
                                    .to_broadcast([P, 2, 2, R])
                            nc.vector.tensor_copy(blocks_of[:, k, :, 0, :, :], four(vh).bitcast(F32))
                            last = nc.vector.tensor_tensor(blocks_of[:, k, :, 1, :, :], four(vf),
                                                           four(vh).bitcast(F32), ALU.subtract)
                        last.then_inc(v_ready, 1)
                    elif s.name == "factors":
                        dve.wait_ge(loaded["u"], 16)
                        then(nc.vector.tensor_tensor(us[:, :, :], u_in[:, :, :],
                                                     fc_inv[:, :].rearrange("p (t a) -> p t a", a=1)
                                                     .to_broadcast([P, HT, R]), ALU.mult))
                        then(nc.vector.tensor_copy(uh[:, :, :], us[:, :, :]))
                        then(nc.vector.tensor_tensor(ul[:, :, :], us[:, :, :], uh[:, :, :].bitcast(F32),
                                                     ALU.subtract))
                        pairs = u_nat[:, :, :].rearrange("p t (m two r) -> p t m two r", two=2, r=R)
                        for n, part_of_u in enumerate((uh, ul)):
                            last = nc.vector.tensor_copy(
                                pairs[:, :, :, n, :],
                                part_of_u[:, :, :].rearrange("p t (m r) -> p t m r", m=1)
                                .to_broadcast([P, HT, P // (2 * R), R]).bitcast(F32))
                        last.then_inc(u_ready, 1)
                    elif s.name == "weights" and s.number in LOW_BLOCKS:
                        n = s.number
                        dve.wait_ge(blocks_copied, n + 1)
                        nc.vector.tensor_tensor(LOW_BLOCKS[n], bank[BLOCK_BANK[n]][:, :],
                                                blocks(n)[1].bitcast(F32), ALU.subtract).then_inc(lows_copied, 1)
                    elif s.name == "masks":
                        nc.vector.tensor_copy(tri[:, :], tri_f[:, :])
                        nc.vector.tensor_scalar(rest[:, :], tri_f[:, :], -1.0, 1.0, ALU.mult, ALU.add)
                        nc.vector.memset(yh[:, :, D + 1:D + 2].bitcast(F32), 0.0)
                        nc.vector.memset(yl[:, :, D + 1:D + 2].bitcast(F32), 0.0).then_inc(masks_done, 1)
                        dve.wait_ge(loaded["b2"], 16)
                        dve.wait_ge(loaded["bc"], 16)
                    elif s.name == "stats":
                        q, src = s.prep, tokens(s)
                        if s.kind == "A":
                            wait(dve, x_loaded[s.half], 16 * (s.batch + 1))
                        elif s.kind == "B":
                            wait(dve, added, 2 * (s.group + 1))
                        else:
                            wait(dve, x2_ready, s.chunks)
                        wait(dve, moments_done, q)
                        for c in range(GC):
                            last = nc.vector.bn_stats(bn[:, c, :], src[:, c, :])
                        last.then_inc(stats_done, 1)
                        wait(dve, xn_ready, q - 1)
                        wait_apart(dve, (const_done, 2), (stats_done, q + 1))
                        for c in range(GC):
                            last = nc.vector.bn_aggr(moments[q.ring(2)][:, c, :], bn[:, c, :])
                        last.then_inc(moments_done, 1)
                    elif s.name == "turn":
                        for k in range(KT):
                            high, low = halves(s, k)
                            wait(dve, hi_done, 2 * s.prep + k + 1)
                            nc.vector.tensor_tensor(low, turned_bank[k][:, :], high.bitcast(F32), ALU.subtract)\
                                .then_inc(turn_taken, 1)
                    elif s.name == "z":
                        low = zt[s.group.ring(2)][P // 2:P, :]
                        wait(dve, zh_done, s.group + 1)
                        nc.vector.tensor_tensor(low, work[s.bank][P // 2:P, :], low.bitcast(F32), ALU.subtract)\
                            .then_inc(zl_done, 1)
                    elif s.name == "square":
                        t = s.tile
                        if s.j % 2 == 0:
                            wait(dve, relu_done, t + 1)
                            if t.each or t.first >= 2:
                                wait(dve, r2l_done, t - 1)
                            nc.vector.tensor_tensor(sq[0][:, :], r[0][:, :], r[0][:, :],
                                                    ALU.mult).then_inc(sq_done, 1)
                            wait(dve, r2h_done, t + 1)
                            wait(dve, sq_done, s.evens + 1)
                        else:
                            wait(dve, act_sq_done, s.evens + 1)
                        nc.vector.tensor_tensor(r2l[t.ring(4)][:, :], sq[t.ring(2)][:, :],
                                                r2h[t.ring(4)][:, :].bitcast(F32), ALU.subtract)\
                            .then_inc(r2l_done, 1)
                    elif s.name == "land":
                        g = s.group
                        if g.is_zero:
                            dve.wait_ge(blocks_copied, ALL_BLOCKS)
                        for h in range(2):
                            wait(dve, down_done, 2 * (HT * g + HT - 1) + h + 1)
                            if g.each or g.first >= 1:
                                wait(dve, added, 2 * g + h - 1)
                            nc.vector.tensor_tensor(ffn[h][:, :, :],
                                                    acc[h][:, :].rearrange("p (c d) -> p c d", c=2),
                                                    proj_row[:, :, :], ALU.mult).then_inc(landed, 1)
                    elif s.name == "score":
                        wait(dve, score_done, s.number + 1)
                        wait(dve, exp_done, s.batch)
                        nc.vector.tensor_scalar(s_all[:, s.half * GC:(s.half + 1) * GC], work[s.bank][:, 0:GC],
                                                b2b[:, 0:1], None, ALU.add).then_inc(scored, 1)
                    elif s.name == "peak":
                        wait(dve, scored, 2 * (s.batch + 1))
                        nc.vector.reduce_max(row_max[:, :], s_all[:, :], AX_X).then_inc(rowmax_done, 1)
                    elif s.name == "exp":
                        wait(dve, eh_done, s.batch + 1)
                        nc.vector.tensor_tensor(yl[:, :, D:D + 1], e[:, :].rearrange("p (c a) -> p c a", a=1),
                                                yh[:, :, D:D + 1].bitcast(F32), ALU.subtract).then_inc(el_done, 1)
                    elif s.name == "mix":
                        m, c = s.chunk, s.c
                        wait(dve, yh_done, m + 1)
                        nc.vector.scalar_tensor_tensor(yl[:, c, 0:D], mix_bank[:, 0:D], e[:, c:c + 1],
                                                       yh[:, c, 0:D].bitcast(F32), ALU.mult, ALU.subtract)\
                            .then_inc(yl_done, 1)
                        nc.vector.tensor_tensor(own[c % 2][:, :], mix_bank[:, D:2 * D], bcb[:, :], ALU.add)\
                            .then_inc(own_done, 1)
                    elif s.name == "sum":
                        m, c = s.chunk, s.c
                        wait(dve, sum_done, m + 1)
                        wait(dve, pre_done, m)
                        nc.vector.reciprocal(rden[:, :], sum_bank[:, D:D + 1]).then_inc(rden_done, 1)
                        wait(dve, gate_done, m - 1)
                        wait(dve, own_done, m + 1)
                        wait(dve, rden_done, m + 1)
                        nc.vector.scalar_tensor_tensor(pre[c % 2][:, :], sum_bank[:, 0:D], rden[:, 0:1],
                                                       own[c % 2][:, :], ALU.mult, ALU.add).then_inc(pre_done, 1)
            run_parts(dve, do)

        @block.tensor
        def _(pe):
            def do(steps, part):
                for s in steps:
                    if s.name == "factors" and s.number == 0:
                        pe.wait_ge(loaded["v"], 16)
                        pe.wait_ge(loaded["fast_b"], 16)
                        for k in range(KT):
                            last = nc.tensor.matmul(bank[5][:, k * R:(k + 1) * R], v_in[:, k * P:(k + 1) * P],
                                                    fbT_in[:, :], start=(k == 0), stop=True,
                                                    skip_group_check=True)
                        last.then_inc(vf_psum, 1)
                    elif s.name == "weights":
                        n = s.number
                        if n == 0:
                            pe.wait_ge(const_done, 2)
                        if n < 4:
                            pe.wait_ge(signs_done, n // 2 + 1)
                        elif n < 6:
                            pe.wait_ge(u_ready, 1)
                        elif n < 10:
                            pe.wait_ge(signs_done, 3)
                        elif n < 11:
                            pe.wait_ge(wide_ready, 1)
                        else:
                            pe.wait_ge(loaded["W1" if n == 11 else "Wc"], 16)
                        if n >= 6:
                            pe.wait_ge(blocks_copied, n - 1)
                        if n - 2 in LOW_BLOCKS:
                            pe.wait_ge(lows_copied, 1)
                        for m, src in enumerate(blocks(n)[0]):
                            last = nc.tensor.transpose(bank[BLOCK_BANK[n]][:, m * P:(m + 1) * P], src, ident[:, :])
                        last.then_inc(blocks_done, 1)
                    elif s.name == "turn":
                        q = s.prep
                        wait(pe, xn_ready, q + 1)
                        for k in range(KT):
                            wait(pe, turn_taken, 2 * q + k - 1)
                            for c in range(GC):
                                last = nc.tensor.transpose(turned_bank[k][:, c * P:(c + 1) * P],
                                                           xn[q.ring(2)][:, c, k * P:(k + 1) * P], ident[:, :])
                            last.then_inc(turned, 1)
                    elif s.name == "z":
                        n = s.group.ring(2)
                        if s.group.is_zero:
                            pe.wait_ge(v_ready, 1)
                            pe.wait_ge(blocks_copied, UP_BLOCKS)
                        claim(pe, s.before)
                        for k in range(KT):
                            wait(pe, turn_taken, 2 * s.prep + k + 1)
                            for x_half in (xh, xl):
                                last = nc.tensor.matmul(work[s.bank][:, :], V[:, k, :], x_half[n][:, k, :],
                                                        start=(k == 0 and x_half is xh),
                                                        stop=(k == KT - 1 and x_half is xl))
                        last.then_inc(z_done, 1)
                    elif s.name == "up":
                        n = s.group.ring(2)
                        cols = slice(s.j * P, (s.j + 1) * P)
                        claim(pe, s.before)
                        for k in range(KT):
                            for x_half in (xh, xl):
                                nc.tensor.matmul(work[s.bank][:, :], fcT[:, k, cols], x_half[n][:, k, :],
                                                 start=(k == 0 and x_half is xh), stop=False)
                        if s.j == 0:
                            wait(pe, zl_done, s.group + 1)
                        nc.tensor.matmul(work[s.bank][:, :], U[:, cols], zt[n][:, :], start=False, stop=True)\
                            .then_inc(up_done, 1)
                    elif s.name == "down":
                        t, g = s.tile, s.group
                        wait(pe, r2l_done, t + 1)
                        if t.is_zero:
                            pe.wait_ge(blocks_copied, DOWN_BLOCKS)
                        for c in range(GC):
                            if s.j == 0 and c % 2 == 0 and (g.each or g.first >= 1):
                                wait(pe, landed, 2 * g + c // 2 - 1)
                            for half in (r2h, r2l):
                                last = nc.tensor.matmul(acc[c // 2][:, (c % 2) * D:(c % 2 + 1) * D],
                                                        half[t.ring(4)][:, c * P:(c + 1) * P], projT[:, s.j, :],
                                                        start=(s.j == 0 and c % 2 == 0 and half is r2h),
                                                        stop=(s.j == HT - 1 and half is r2l),
                                                        skip_group_check=True)
                            if c % 2 == 1:
                                last.then_inc(down_done, 1)
                    elif s.name == "hidden":
                        if s.number.is_zero:
                            pe.wait_ge(blocks_copied, ALL_BLOCKS)
                            pe.wait_ge(lows_copied, len(LOW_BLOCKS))
                            pe.wait_ge(loaded["w2"], 16)
                            pe.wait_ge(masks_done, 1)
                        claim(pe, s.before)
                        cols, rows = slice(s.half * G, (s.half + 1) * G), slice(s.e * P, (s.e + 1) * P)
                        products = [(w, t, k) for k in range(KT) for w, t in ((W1h, xnTh), (W1h, xnTl), (W1l, xnTh))]
                        for w, t, k in products:
                            if (w, t) == (W1h, xnTh):
                                wait(pe, turn_taken, 2 * s.prep + k + 1)
                            last = nc.tensor.matmul(work[s.bank][:, :], w[:, k, rows], t[:, k, cols],
                                                    start=((w, t, k) == products[0]),
                                                    stop=((w, t, k) == products[-1]))
                        last.then_inc(hid_done, 1)
                    elif s.name == "score":
                        wait(pe, tanh_done, 2 * (s.number + 1))
                        claim(pe, s.before)
                        for c in range(GC):
                            for k in range(KT):
                                last = nc.tensor.matmul(work[s.bank][:, c:c + 1], hT[:, k, c * P:(c + 1) * P],
                                                        w2c[:, k:k + 1], start=(c == 0 and k == 0),
                                                        stop=(k == KT - 1), skip_group_check=True)
                        last.then_inc(score_done, 1)
                    elif s.name == "mix":
                        wait(pe, own_done, s.chunk)
                        cols = slice(s.c * P, (s.c + 1) * P)
                        products = [(t, w, k) for k in range(KT) for t, w in ((xnTh, Wch), (xnTh, Wcl), (xnTl, Wch))]
                        for t, w, k in products:
                            last = nc.tensor.matmul(mix_bank[:, :], t[:, k, cols], w[:, k, :],
                                                    start=((t, w, k) == products[0]),
                                                    stop=((t, w, k) == products[-1]))
                        last.then_inc(mix_done, 1)
                    elif s.name == "sum":
                        wait(pe, yl_done, s.chunk + 1)
                        if s.c == 0:
                            wait(pe, el_done, s.batch + 1)
                            wait(pe, pre_done, s.chunk)
                        for half in (yh, yl):
                            last = nc.tensor.matmul(sum_bank[:, 0:NY], tri[:, :], half[:, s.c, :],
                                                    start=(s.c == 0 and half is yh), stop=(half is yl),
                                                    skip_group_check=True)
                        last.then_inc(sum_done, 1)
                    elif s.name == "carry":
                        wait(pe, pre_done, s.chunk + 1)
                        for half in (yh, yl):
                            nc.tensor.matmul(sum_bank[:, 0:NY], rest[:, :], half[:, s.c, :], start=False,
                                             stop=(half is yl), skip_group_check=True)
            run_parts(pe, do)
_INS = ['L0_attn_x', 'L0_attn_W1', 'L0_attn_b1', 'L0_attn_w2', 'L0_attn_b2', 'L0_attn_Wc', 'L0_attn_bc',
        'L0_ffn_fast_b', 'L0_ffn_w_fc', 'L0_ffn_w_proj', 'L0_ffn_u', 'L0_ffn_v', 'L0_ffn_gate']


def kernel(**inputs):
    import numpy as _np
    import concourse.bacc as _bacc
    from concourse import mybir as _mybir
    from concourse.bass_utils import run_bass_kernel_spmd as _run

    nc = _bacc.Bacc("TRN2", target_bir_lowering=False, num_devices=1)
    arrays, args = {}, []
    for name in _INS:
        a = _np.ascontiguousarray(inputs[name])
        if a.ndim == 0:
            a = a.reshape(1)
        arrays[f"in_{name}_dram"] = a
        args.append(nc.dram_tensor(f"in_{name}_dram", a.shape, _mybir.dt.from_np(a.dtype), kind="ExternalInput").ap())
    args.append(nc.dram_tensor("out_0_dram", (B, T, D), _mybir.dt.float32, kind="ExternalOutput").ap())
    macaron(nc, *args)
    r = _run(nc, [arrays], core_ids=[0])
    return r.results[0]["out_0_dram"]
```
